# Optimizing a Trainium2 kernel written in Bass

```python
import numpy as np
import jax
import jax.numpy as jnp

def _softmax(x, axis=-1):
    return jax.nn.softmax(x, axis=axis)

def _gelu(x):
    return jax.nn.gelu(x, approximate=True)

def _silu(x):
    return jax.nn.silu(x)

def _sigmoid(x):
    return jax.nn.sigmoid(x)

def _layernorm(x, axis=-1, eps=1e-05):
    m = jnp.mean(x, axis=axis, keepdims=True)
    v = jnp.var(x, axis=axis, keepdims=True)
    return (x - m) / jnp.sqrt(v + eps)

def _scatter_add(tgt, idx, src, axis=0):
    return tgt.at[idx].add(src)

def _segment_sum(src, seg, n):
    return jax.ops.segment_sum(src, seg, n)
kernel_name = 'mk_early_fusion_d1_tok_img1024_r4_e9d396'

def setup_inputs(seed: int=0):
    np.random.seed(seed)
    _w = jnp.asarray

    def _rec_inputs():
        import jax
        import jax.numpy as jnp
        _rk = jax.random.key(seed)
        x = -0.000221324 + 1.00063 * jax.random.normal(jax.random.fold_in(_rk, 1), (4, 64, 64, 3), jnp.float32)
        txt = -0.00173256 + 0.381199 * jax.random.normal(jax.random.fold_in(_rk, 2), (4, 128, 256), jnp.float32)
        return (x, txt)
    x, txt = _rec_inputs()

    def _L0_tok_setup():
        import jax, jax.numpy as jnp
        import numpy as np
        NUM_STEPS = 16
        D_MODEL = 256
        key = jax.random.key(seed)
        k1, k2 = jax.random.split(key)
        B, H, W, C = (32, 64, 64, 3)
        path_params_grid = jax.random.normal(k1, (B, H, W, C), dtype=jnp.float32)
        kernel = jax.random.normal(k2, (2, D_MODEL), dtype=jnp.float32) * (1.0 / np.sqrt(2.0))
        bias = jnp.zeros((D_MODEL,), dtype=jnp.float32)
        return {'path_params_grid': path_params_grid, 'kernel': kernel, 'bias': bias}
    _L0_tok_all = _L0_tok_setup()
    _L0_tok_in = {k: v for k, v in _L0_tok_all.items() if k in ('kernel', 'bias')}
    del _L0_tok_all

    def _L0_attn_setup():
        import jax, jax.numpy as jnp
        import numpy as np
        HEADS = 16
        NUM_LANDMARKS = 64
        PINV_ITERS = 6
        D_MODEL = 256

        def _moore_penrose_pinv(x, num_iters):
            m = x.shape[-1]
            I = jnp.eye(m, dtype=x.dtype)
            V = x
            for _ in range(num_iters):
                KV = x @ V
                V = 0.25 * V @ (13.0 * I - KV @ (15.0 * I - KV @ (7.0 * I - KV)))
            return V
        key = jax.random.key(seed)
        k1, k2, k3 = jax.random.split(key, 3)
        b, n, d = (4, 1024, D_MODEL)
        hidden_states = jax.random.normal(k1, (b, n, d), dtype=jnp.float32)
        Wqkv = jax.random.normal(k2, (d, 3 * d), dtype=jnp.float32) * 0.02
        bqkv = jnp.zeros((3 * d,), dtype=jnp.float32)
        Wout = jax.random.normal(k3, (d, d), dtype=jnp.float32) * 0.02
        bout = jnp.zeros((d,), dtype=jnp.float32)
        return {'hidden_states': hidden_states, 'Wqkv': Wqkv, 'bqkv': bqkv, 'Wout': Wout, 'bout': bout}
    _L0_attn_all = _L0_attn_setup()
    _L0_attn_in = {k: v for k, v in _L0_attn_all.items() if k in ('Wqkv', 'bqkv', 'Wout', 'bout')}
    del _L0_attn_all

    def _L0_ffn_setup():
        import jax, jax.numpy as jnp
        import numpy as np
        SL, BS, HS = (512, 4, 256)
        FF = 1024
        E, RANK, TOPK = (8, 64, 2)
        key = jax.random.key(seed)
        ks = jax.random.split(key, 7)
        s = 0.02
        return {'x': jax.random.normal(ks[0], (SL, BS, HS), jnp.float32), 'expert_weights': jax.random.uniform(ks[1], (SL * BS, TOPK), jnp.float32), 'expert_indices': jax.random.randint(ks[2], (SL * BS, TOPK), 0, E).astype(jnp.int32), 'w1_A': jax.random.normal(ks[3], (E * RANK, HS), jnp.float32) * s, 'w1_B': jax.random.normal(ks[4], (E * RANK, FF), jnp.float32) * s, 'w2_A': jax.random.normal(ks[5], (E * RANK, FF), jnp.float32) * s, 'w2_B': jax.random.normal(ks[6], (E * RANK, HS), jnp.float32) * s}
    _L0_ffn_all = _L0_ffn_setup()
    _L0_ffn_in = {k: v for k, v in _L0_ffn_all.items() if k in ('expert_weights', 'expert_indices', 'w1_A', 'w1_B', 'w2_A', 'w2_B')}
    del _L0_ffn_all
    return {'x': x, 'txt': txt, 'L0_tok_kernel': _L0_tok_in['kernel'], 'L0_tok_bias': _L0_tok_in['bias'], 'L0_attn_Wqkv': _L0_attn_in['Wqkv'], 'L0_attn_bqkv': _L0_attn_in['bqkv'], 'L0_attn_Wout': _L0_attn_in['Wout'], 'L0_attn_bout': _L0_attn_in['bout'], 'L0_ffn_expert_weights': _L0_ffn_in['expert_weights'], 'L0_ffn_expert_indices': _L0_ffn_in['expert_indices'], 'L0_ffn_w1_A': _L0_ffn_in['w1_A'], 'L0_ffn_w1_B': _L0_ffn_in['w1_B'], 'L0_ffn_w2_A': _L0_ffn_in['w2_A'], 'L0_ffn_w2_B': _L0_ffn_in['w2_B']}

def reference(x, txt, L0_tok_kernel, L0_tok_bias, L0_attn_Wqkv, L0_attn_bqkv, L0_attn_Wout, L0_attn_bout, L0_ffn_expert_weights, L0_ffn_expert_indices, L0_ffn_w1_A, L0_ffn_w1_B, L0_ffn_w2_A, L0_ffn_w2_B):
    import jax
    import jax.numpy as jnp

    def _L0_tok_ref(path_params_grid, kernel, bias):
        import jax, jax.numpy as jnp
        import numpy as np
        NUM_STEPS = 16
        D_MODEL = 256
        B, H, W, C = path_params_grid.shape
        L = H * W
        p = path_params_grid.reshape(B, L, C)
        delta_c, chi_c, radius = (p[..., 0], p[..., 1], p[..., 2])
        theta = jnp.linspace(0.0, 2.0 * jnp.pi, NUM_STEPS, dtype=jnp.float32)
        delta_path = delta_c[..., None] + radius[..., None] * jnp.cos(theta)
        chi_path = chi_c[..., None] + radius[..., None] * jnp.sin(theta)
        re = jnp.cos(delta_path / 2)
        im = jnp.sin(delta_path / 2) * jnp.sin(2 * chi_path)
        t = re + 1j * im
        acc = jnp.prod(t, axis=-1)
        meas = jnp.stack([acc.real, acc.imag], axis=-1)
        return meas @ kernel + bias

    def _L0_attn_ref(hidden_states, Wqkv, bqkv, Wout, bout):
        import jax, jax.numpy as jnp
        import numpy as np
        HEADS = 16
        NUM_LANDMARKS = 64
        PINV_ITERS = 6
        D_MODEL = 256

        def _moore_penrose_pinv(x, num_iters):
            m = x.shape[-1]
            I = jnp.eye(m, dtype=x.dtype)
            V = x
            for _ in range(num_iters):
                KV = x @ V
                V = 0.25 * V @ (13.0 * I - KV @ (15.0 * I - KV @ (7.0 * I - KV)))
            return V
        b, n, d = hidden_states.shape
        h, m = (HEADS, NUM_LANDMARKS)
        dh = d // h
        scale = 1.0 / np.sqrt(dh).astype(np.float32)
        l = n // m
        qkv = hidden_states @ Wqkv + bqkv
        q, k, v = jnp.split(qkv, 3, axis=-1)

        def to_heads(t):
            return t.reshape(b, n, h, dh).transpose(0, 2, 1, 3)
        q, k, v = (to_heads(q), to_heads(k), to_heads(v))
        q = q * scale
        q_l = q.reshape(b, h, m, l, dh).mean(axis=3)
        k_l = k.reshape(b, h, m, l, dh).mean(axis=3)
        sim1 = jnp.einsum('bhid,bhjd->bhij', q, k_l)
        sim2 = jnp.einsum('bhid,bhjd->bhij', q_l, k_l)
        sim3 = jnp.einsum('bhid,bhjd->bhij', q_l, k)
        attn1 = jax.nn.softmax(sim1, axis=-1)
        attn2 = jax.nn.softmax(sim2, axis=-1)
        attn3 = jax.nn.softmax(sim3, axis=-1)
        attn2_inv = _moore_penrose_pinv(attn2, PINV_ITERS)
        out = attn1 @ (attn2_inv @ (attn3 @ v))
        out = out.transpose(0, 2, 1, 3).reshape(b, n, d)
        out = out @ Wout + bout
        return out

    def _L0_ffn_ref(x, expert_weights, expert_indices, w1_A, w1_B, w2_A, w2_B):
        import jax, jax.numpy as jnp
        import numpy as np
        SL, BS, HS = (512, 4, 256)
        FF = 1024
        E, RANK, TOPK = (8, 64, 2)
        sl, bs, hs = x.shape
        T = sl * bs
        top_k = expert_indices.shape[-1]
        flat_e = expert_indices.reshape(-1)
        flat_w = expert_weights.reshape(-1)
        order = jnp.argsort(flat_e, stable=True)
        bin_ids = flat_e[order]
        tok = order // top_k
        xr = x.reshape(T, hs)[tok]
        w1A = w1_A.reshape(E, RANK, hs)
        w1B = w1_B.reshape(E, RANK, FF)
        w2A = w2_A.reshape(E, RANK, FF)
        w2B = w2_B.reshape(E, RANK, hs)
        out = jnp.zeros_like(xr)
        for e in range(E):
            mask = (bin_ids == e).astype(xr.dtype)[:, None]
            h = jax.nn.gelu(xr @ w1A[e].T @ w1B[e], approximate=False)
            ye = h @ w2A[e].T @ w2B[e]
            out = out + mask * ye
        y = jnp.zeros((T, hs), xr.dtype).at[tok].add(flat_w[order][:, None] * out)
        return y.reshape(sl, bs, hs)
    h = _L0_tok_ref(x, L0_tok_kernel, L0_tok_bias)
    h = jnp.concatenate([h, txt], axis=1)
    h = h + _L0_attn_ref(_layernorm(h, axis=-1), L0_attn_Wqkv, L0_attn_bqkv, L0_attn_Wout, L0_attn_bout)
    h = h + _L0_ffn_ref(_layernorm(h, axis=-1), L0_ffn_expert_weights, L0_ffn_expert_indices, L0_ffn_w1_A, L0_ffn_w1_B, L0_ffn_w2_A, L0_ffn_w2_B)
    return h

_drawn_inputs = setup_inputs


def setup_inputs(seed=0):
    import zlib

    import numpy as np

    out = dict(_drawn_inputs(seed))
    spreads = {'L0_tok_bias': (0.0, 0.1), 'L0_attn_bqkv': (0.0, 0.1), 'L0_attn_bout': (0.0, 0.1)}
    factors = {'L0_ffn_expert_weights': 8.0,
     'L0_ffn_w1_A': 8.0,
     'L0_ffn_w1_B': 8.0,
     'L0_ffn_w2_A': 8.0,
     'L0_ffn_w2_B': 8.0,
     'txt': 30.927}
    for name, (base, spread) in spreads.items():
        noise = np.random.default_rng([zlib.crc32(name.encode()), seed]).standard_normal(out[name].shape)
        drawn = base * np.exp(spread * noise) if base else spread * noise
        out[name] = jnp.asarray(drawn.astype(out[name].dtype))
    for name, factor in factors.items():
        out[name] = (out[name] * factor).astype(out[name].dtype)
    return out
```

```python
import math
from contextlib import ExitStack

import numpy as np
import concourse.bass as bass
from concourse import mybir

F32 = mybir.dt.float32
BF16 = mybir.dt.bfloat16
ALU = mybir.AluOpType
ACT = mybir.ActivationFunctionType
AX = mybir.AxisListType
ds = bass.ds

P = 128
NB = 4
NG = 4096
NX = 128
NT = NG // P
TILES = NT + 1
CH = NG // 512
D = 256
H = 16
DH = D // H
LM = 64
GROUP = (NG + NX) // LM
STEPS = 16
PAIRS = H // 2
ITERS = 6
EPS = 1e-5
FFN_T = 2048
FT = FFN_T // P
E = 8
RANK = 64
FF = 1024
FB = FF // P

A_COLS = {1: (0, 64, 96), 2: (4, 68), 3: (8,)}
B_COLS = {1: (12, 72, 100), 2: (14, 74), 3: (16,)}
MAXROW = 32
ONEROW = 48
SPLIT_ROWS = (0, 64, 96)

LAYOUT = {}
_at = 0
for _name, _n in (("ident", 128), ("trig", 32), ("mask8", 8), ("sel3", 128), ("sel1", 128), ("e3", 4),
                  ("selV", 256), ("col32", 2), ("onehot", 256), ("negind", 1024), ("selE", 512), ("iota8", 8)):
    LAYOUT[_name] = (_at, _at + _n)
    _at += _n
NCONST = _at


def constants():
    c = np.zeros((P, NCONST), np.float32)

    def part(name):
        a, b = LAYOUT[name]
        return c[:, a:b]

    part("ident")[:] = np.eye(P, dtype=np.float32)
    theta = np.linspace(0.0, 2.0 * np.pi, STEPS, dtype=np.float32).astype(np.float64)
    part("trig")[:, 0:16] = np.cos(theta)
    part("trig")[:, 16:32] = np.sin(theta)
    for ch in range(P):
        part("mask8")[ch, ch // DH] = 1.0
    for n in (1, 2, 3):
        for col in B_COLS[n]:
            part("sel3")[0, col] = 1.0
            part("sel3")[1, col + 1] = 1.0
    for col in A_COLS[1]:
        part("sel3")[2, col + 3] = 1.0
        part("sel1")[0, col + 3] = 1.0
    part("e3")[0, 3] = 1.0
    sel_v = part("selV").reshape(P, 2, 128)
    for half in range(2):
        for k in range(4):
            for q in (half, half + 2):
                sel_v[k, half, 32 * q + k] = 1.0
        for q in (half, half + 2):
            part("col32")[32 * q + 3, half] = 1.0
    one = part("onehot").reshape(P, PAIRS, 32)
    for p in range(PAIRS):
        one[0:64, p, 2 * p] = 1.0
        one[64:128, p, 2 * p + 1] = 1.0
    neg = part("negind").reshape(P, H, LM)
    for h in range(H):
        neg[MAXROW + h, h, :] = -1.0
    sel_e = part("selE").reshape(P, 4, 128)
    for e in range(E):
        sel_e[e, e // 2, 64 * (e % 2):64 * (e % 2) + 64] = 1.0
    part("iota8")[:] = np.arange(E, dtype=np.float32)
    member = np.zeros((P, TILES, LM), np.float32)
    for n in range(TILES):
        for p in range(P):
            token = NG + p if n == NT else (n // 16) * 2048 + p * 16 + n % 16
            member[p, n, token // GROUP] = 1.0 / GROUP
    return c, member.reshape(P, TILES * LM)


def build(nc, x, txt, tok_kernel, tok_bias, wqkv, bqkv, wout, bout, ew, ei, w1a_t, w1b, w2a_t, w2b,
          consts, member, out):
    ctx = ExitStack()
    with ctx:
        def sb(name, shape, dt=F32):
            return ctx.enter_context(nc.sbuf_tensor(name, shape, dt))

        def sem(name):
            return ctx.enter_context(nc.semaphore(name))

        ps = ctx.enter_context(nc.psum_tensor("ps", [P, 8, 512], F32))

        def psb(i):
            return ps[:, i, :].bitcast(BF16)

        arena = sb("arena", [P, 18432])
        taken = [0]

        def view(shape, dt=F32):
            n = int(np.prod(shape[1:]))
            words = n if dt == F32 else n // 2
            v = arena[:, taken[0]:taken[0] + words]
            taken[0] += words
            if dt != F32:
                v = v.bitcast(dt)
            if len(shape) == 3:
                v = v.rearrange("p (a b) -> p a b", b=shape[2])
            if len(shape) == 4:
                v = v.rearrange("p (a b c) -> p a b c", b=shape[2], c=shape[3])
            return v

        sb_const = sb("sb_const", [P, NCONST])
        sb_member = sb("sb_member", [P, TILES, LM])

        def con(name):
            a, b = LAYOUT[name]
            return sb_const[:, a:b]

        ident = con("ident")
        identb = sb("identb", [P, P], BF16)
        eps_col = sb("eps_col", [P, 1])
        halfpi = sb("halfpi", [P, 1])
        waiter = sb("waiter", [P, 1])
        ones_row = sb("ones_row", [1, P])
        mean_w = sb("mean_w", [P, P])
        wq = sb("wq", [P, 2, 3 * D])
        bq = sb("bq", [1, 3 * D])
        wo = sb("wo", [P, 2, D])
        kb = sb("kb", [3, D])
        kbc = sb("kbc", [3, D])
        ksum = sb("ksum", [3, 2])
        bo = sb("bo", [1, D])
        bout_all = sb("bout_all", [P, D])
        kt4 = sb("kt4", [P, 2, 4])
        prod = sb("prod", [P, 2, 6])
        gram = sb("gram", [P, 6])
        m4 = sb("m4", [4, 3 * D])
        mt = sb("mt", [P, 4, P])
        v4x = sb("v4x", [P, PAIRS, 34])
        split_r = sb("split_r", [P, 512])
        res_w = sb("res_w", [P, D], BF16)
        xb = sb("xb", [P, NT, 3])
        ang = [view([P, NT, STEPS]) for _ in range(2)]
        rnd = [view([P, NT, STEPS]) for _ in range(2)]
        sin_a = view([P, NT, STEPS])
        abs_a = view([P, NT, STEPS])
        re = view([P, NT, STEPS])
        im = view([P, NT, STEPS])
        tre = view([P, 4, NT, 8])
        st = sb("st", [P, 4, NT])
        reim = sb("reim", [P, NT, 2])
        sd = sb("sd", [P, NT])
        rstd = sb("rstd", [P, NT])
        cf = sb("cf", [P, TILES, 32])
        ce = sb("ce", [P, NT, 4])
        tc = view([P, TILES, P], BF16)
        coef_t = sb("coef_t", [P, TILES * P], BF16)
        tx = sb("tx", [P, D])
        txr = sb("txr", [P, D])
        txn = sb("txn", [P, D])
        txstat = sb("txstat", [P, 6])
        txmv = sb("txmv", [P, 2])
        txsd = sb("txsd", [P, 2])
        txn_t = sb("txn_t", [P, 2, P])
        qkv_x = sb("qkv_x", [P, 3 * D])
        qk_xt = sb("qk_xt", [P, 4, P])
        lm_c = sb("lm_c", [4, LM])
        klt = sb("klt", [P, 2, LM])
        kl_bd = sb("kl_bd", [P, 2, 8, LM])
        ql_bd = sb("ql_bd", [P, 2, 8, LM])
        g1 = sb("g1", [P, H * LM], BF16)
        g3 = sb("g3", [P, H * LM], BF16)
        s2 = sb("s2", [P, PAIRS, LM])
        s2m = sb("s2m", [P, 2, PAIRS])
        bd = [P, PAIRS, P]
        xbd, xt, ym, yt, y2t, qm, vt, ylin, y7 = (
            view(bd) for _ in range(9))
        id7 = sb("id7", [P, P])
        id13 = sb("id13", [P, P])
        m3part = sb("m3part", [P, PAIRS, 5])
        m3z = sb("m3z", [P, PAIRS, 32])
        c3 = sb("c3", [P, 512])
        w3 = sb("w3", [P, PAIRS, DH])
        w3r = sb("w3r", [P, PAIRS])
        z_bd = sb("z_bd", [P, PAIRS, 32])
        prob = sb("prob", [P, 2, 4, 512])
        p3 = prob[:, :, :, :].rearrange("p a b c -> p (a b c)").rearrange("p (n c) -> p n c", n=4)
        p1 = prob
        cfw = sb("cfw", [P, 8, 32])
        m1 = sb("m1", [P, 4, H], BF16)
        u_sb = sb("u_sb", [P, 2, 2, 512])
        d_sb = sb("d_sb", [P, 512])
        d_t = sb("d_t", [P, 4, H])
        rd = sb("rd", [P, 4, H])
        rd_all = sb("rd_all", [P, 4, H, DH])
        o_sb = sb("o_sb", [P, 2, 512])
        out_sb = sb("out_sb", [P, 2, 4, D])

        taken[0] = 0
        w1b_z = view([P, E, FF])
        w2a_s = view([P, FB, E * RANK])
        w2b_s = view([P, E // 2, D])
        w1a_s = view([P, 2, E * RANK])
        x1 = view([P, FT, D])
        assert taken[0] == 18432
        spare = prob[:, :, :, :].rearrange("p a b c -> p (a b) c")
        hid = spare[:, 0:4, :].rearrange("p (e r) c -> p e r c", e=2)
        y2 = spare[:, 4:8, :]
        mid = u_sb[:, :, :, :].rearrange("p a b c -> p (a b) c")
        xn = kl_bd[:, :, :, :].rearrange("p a h j -> p (a h j)").rearrange("p (n c) -> p n c", n=4)
        xn_t = rd_all[:, :, :, :].rearrange("p n h d -> p (n h d)").rearrange("p (k c) -> p k c", k=2)
        wx = split_r
        we_t = coef_t[:, 0:2 * FFN_T].bitcast(F32)
        ew_s = sb("ew_s", [P, FT, 2])
        ei_s = sb("ei_s", [P, FT, 2], mybir.dt.int32)
        ei_f = sb("ei_f", [P, FT, 2])
        eq = txn[:, :].rearrange("p (k n e) -> p k n e", k=2, n=FT)
        fst = sb("fst", [P, FT, 6])
        fmv = sb("fmv", [P, FT, 2])
        fsd = sb("fsd", [P, 2, FT])

        s_const = sem("s_const")
        s_w = sem("s_w")
        s_zero = sem("s_zero")
        s_xin = sem("s_xin")
        s_txin = sem("s_txin")
        pool_step = sem("pool_step")
        dve_step = sem("dve_step")
        S = {n: sem(n) for n in """
            kbc_ready kt_ps kt4_ready gram_ps m4_ps m4_sb mt_ps v4_ps resw_ps bout_ps setup_sb gram_sb
            ang_ready sin_ready var_ready sd_ready txvar_ready tc_ready tx_used
            txn_ready txnt_ps txnt_sb coef_ps coef_act coef_dve qkx_ps qkx_sb lm_ps lm_sb qkxt_ps qkxt_sb
            qkl_ps klbd_ready qlbd_ready g_ps g_first g_ready s2_ps s2_sub s2_exp xbd_ready xt_ps xt_sb
            pi_pe0 pi_pe1 pi_act0 pi_act1 pi_dve0 pi_dve1 s3m_pe s3m_used m3_ready m3_ps g3_shift
            s3_pe s3_exp pv3_pe cfw_ready c3_sb o3_ps w3_ready z_ps z_ready
            s1m_pe s1m_used m1t_ps m1t_sb s1_pe p1_ready ud_pe u_ready d_ready dt_ps dt_used rd_ready rdb_ready
            rdt_ps o_ready out_ps out_ready out_stored0 out_stored1
            f_zero f_in f_x f_e f_we f_wet_ps f_wet f_var f_sd f_xn f_xnt_ps f_xnt f_l0 f_mid f_wx_ps f_wx f_l1 f_gelu
            f_l2 f_y2 f_out_ps f_out f_stored""".split()}
        C9 = CH + 1
        NCH = 2 * PAIRS
        PI_PE = 1 + 3 * ITERS
        PI_ACT = 2 + ITERS + 3 * (ITERS - 1) + 1
        PI_DVE = ITERS + ITERS

        G_ORDER = ((g3, 6, 0), (g3, 7, 1), (g1, 2, 0), (g1, 5, 1))

        def first(v):
            return isinstance(v, int) and v == 0

        FROM_ONE = """rdt_ps ud_pe rdb_ready out_ps dt_ps out_stored0 out_stored1 f_stored pi_act0 pi_act1
            pi_dve0 pi_dve1 s3m_used s1m_used u_ready d_ready out_ready""".split()
        started = sb("started", [P, len(FROM_ONE)])

        def past(n):
            return n + 1

        def score_units():
            return [(p, d) for p in range(PAIRS) for d in range(CH // 2)] + [(None, CH // 2)]

        def pinv_steps():
            steps = [("init", 0)] + [(s, k) for k in range(ITERS) for s in ("square", "poly", "next")]
            units = score_units()
            plan = []
            for s, k in steps:
                for half in range(2):
                    plan.append((s, k, half, units[:1]))
                    units = units[1:]
            assert len(units) == 0
            return plan

        block = ctx.enter_context(nc.Block())

        @block.sync
        def _(sp):
            sp.dma_start(sb_const[:, :], consts).then_inc(s_const, 16)

            def load_points(b):
                if not first(b):
                    sp.wait_ge(S["ang_ready"], 2 * b)
                for half in range(2):
                    sp.dma_start(xb[:, 16 * half:16 * half + 16, :],
                                 x[ds(b, 1), half, :, :].rearrange("o p (n c) -> p (o n) c", c=3)).then_inc(s_xin, 16)

            def load_text(b):
                if not first(b):
                    sp.wait_ge(S["tx_used"], b)
                sp.dma_start(tx[:, :], txt[ds(b, 1), :, :].rearrange("o p n -> p (o n)")).then_inc(s_txin, 16)

            load_points(0)
            sp.dma_start(wq[:, :, :], wqkv.rearrange("(k p) n -> p k n", p=P)).then_inc(s_w, 16)
            sp.dma_start(bq[:, :], bqkv).then_inc(s_w, 16)
            sp.dma_start(kb[0:2, :], tok_kernel).then_inc(s_w, 16)
            sp.dma_start(kb[2:3, :], tok_bias).then_inc(s_w, 16)
            sp.dma_start(bo[:, :], bout).then_inc(s_w, 16)
            sp.dma_start(wo[:, :, :], wout.rearrange("(k p) n -> p k n", p=P)).then_inc(s_w, 16)
            sp.dma_start(sb_member[:, :, :], member.rearrange("p (n j) -> p n j", n=TILES)).then_inc(s_w, 16)
            load_text(0)

            def store_path(b, k):
                sp.wait_ge(S["out_ready"], past(2 * (C9 * b + k) + 2))
                rows = out[ds(b, 1), 2048 * (k // 4):2048 * (k // 4) + 2048, :].rearrange(
                    "o (p n) c -> p (o n) c", n=16)
                sp.dma_start(rows[:, 4 * (k % 4):4 * (k % 4) + 4, :], out_sb[:, k % 2, :, :]).then_inc(
                    S[f"out_stored{k % 2}"], 16)

            def stores(b):
                for k in range(CH):
                    store_path(b, k)
                sp.wait_ge(S["out_ready"], past(2 * (C9 * b + CH) + 2))
                sp.dma_start(out[ds(b, 1), NG:NG + NX, :].rearrange("o p c -> p (o c)"),
                             out_sb[:, 0, 0, :]).then_inc(S["out_stored0"], 16)

            with sp.Fori(0, NB - 1) as b:
                load_points(b + 1)
                load_text(b + 1)
                stores(b)
            sp.wait_ge(S["z_ready"], NB)
            for half in range(2):
                w1b_v = w1b.rearrange("(e r) f -> r e f", e=E)
                sp.dma_start(w1b_z[64 * half:64 * half + 64, half:E:2, :], w1b_v[:, half:E:2, :]).then_inc(S["f_in"], 16)
            sp.dma_start(w1a_s, w1a_t.rearrange("(k p) n -> p k n", p=P)).then_inc(S["f_in"], 16)
            sp.dma_start(w2a_s, w2a_t.rearrange("(k p) n -> p k n", p=P)).then_inc(S["f_in"], 16)
            sp.dma_start(w2b_s, w2b.rearrange("(k p) n -> p k n", p=P)).then_inc(S["f_in"], 16)
            sp.dma_start(ew_s[:, :, :], ew.rearrange("p (n k) -> p n k", k=2)).then_inc(S["f_e"], 16)
            sp.dma_start(ei_s[:, :, :], ei.rearrange("p (n k) -> p n k", k=2)).then_inc(S["f_e"], 16)
            sp.wait_ge(S["out_stored0"], past(16 * 5))
            sp.wait_ge(S["out_stored1"], past(16 * 4))
            ffn_rows = out[0:1, 0:FFN_T, :].rearrange("o (p n) c -> p (o n) c", n=FT)
            sp.dma_start(x1, ffn_rows).then_inc(S["f_x"], 16)
            stores(NB - 1)
            sp.wait_ge(S["out_stored0"], past(16 * 5 * NB))
            sp.wait_ge(S["out_stored1"], past(16 * 4 * NB))
            with sp.Fori(0, FT // 4) as c:
                sp.wait_ge(S["f_out"], 2 * c + 2)
                sp.dma_start(ffn_rows[:, ds(4 * c, 4), :], out_sb[:, 0, :, :]).then_inc(S["f_stored"], 16)
            sp.wait_ge(S["f_stored"], past(16 * (FT // 4)))

        @block.gpsimd
        def _(pool):
            POOL_STEPS = 14 + 1 + 24 + 7
            count = [0]

            def waiting():
                pool.tensor_tensor(waiter[:, :], eps_col[:, :], eps_col[:, :], ALU.mult)

            for t in (cf[:, :, :], tc, mt[:, :, :], xbd, m3z[:, :, :], z_bd[:, :, :], kt4[:, :, :], v4x[:, :, :]):
                pool.memset(t, 0.0).then_inc(s_zero, 1)
            pool.memset(eps_col[:, :], EPS).then_inc(s_zero, 1)
            pool.memset(halfpi[:, :], math.pi / 2).then_inc(s_zero, 1)
            pool.memset(ones_row[:, :], 1.0).then_inc(s_zero, 1)
            pool.memset(mean_w[:, :], 1.0 / D).then_inc(s_zero, 1)
            pool.wait_ge(s_zero, 12)
            pool.memset(cf[:, :, 3:4], 1.0).then_inc(s_zero, 1)
            pool.memset(tc[:, :, ONEROW:ONEROW + 1], 1.0).then_inc(s_zero, 1)
            cosb, sinb = (con("trig")[:, 16 * i:16 * i + 16].rearrange("p (o k) -> p o k", o=1).to_broadcast(
                [P, NT, STEPS]) for i in range(2))

            def tokens(b):
                count[0] = 0

                def step(ins, scalar=False):
                    count[0] += 1
                    ins.then_inc(pool_step, 1)
                    pool.wait_ge(pool_step, POOL_STEPS * b + count[0])
                    if scalar:
                        waiting()

                def col(i):
                    return xb[:, :, i:i + 1].to_broadcast([P, NT, STEPS])

                pool.wait_ge(s_xin, 32 * b + 32)
                magic = 1.5 * 2.0 ** 23
                for i, (trig, period) in enumerate(((cosb, 4 * math.pi), (sinb, math.pi))):
                    a = ang[i][:, :, :]
                    c1 = math.floor(period * 32) / 32
                    step(pool.tensor_tensor(a, col(2), trig, ALU.mult))
                    step(pool.tensor_tensor(a, a, col(i), ALU.add), True)
                    step(pool.tensor_scalar(rnd[0][:, :, :], a, 1.0 / period, magic, ALU.mult, ALU.add), True)
                    step(pool.tensor_scalar(rnd[1][:, :, :], rnd[0][:, :, :], -magic, -c1, ALU.add, ALU.mult))
                    step(pool.tensor_tensor(a, a, rnd[1][:, :, :], ALU.add), True)
                    step(pool.tensor_scalar(rnd[1][:, :, :], rnd[0][:, :, :], -magic, c1 - period, ALU.add, ALU.mult))
                    step(pool.tensor_tensor(a, a, rnd[1][:, :, :], ALU.add), True)
                    lim = float(np.nextafter(np.float32(period / 2), np.float32(0)))
                    pool.tensor_scalar(a, a, lim, -lim, ALU.min, ALU.max).then_inc(S["ang_ready"], 1)
                pool.wait_ge(S["sin_ready"], 4 * b + 4)
                step(pool.tensor_tensor(im[:, :, :], sin_a[:, :, :], im[:, :, :], ALU.mult))
                w = STEPS // 2
                while w:
                    last = w == 1
                    r0, r1, i0, i1 = re[:, :, 0:w], re[:, :, w:2 * w], im[:, :, 0:w], im[:, :, w:2 * w]
                    t = [tre[:, j, :, 0:w] for j in range(4)]
                    for o, (p_, q_) in zip(t, ((r0, r1), (i0, i1), (r0, i1), (i0, r1))):
                        step(pool.tensor_tensor(o, p_, q_, ALU.mult))
                    if last:
                        if not first(b):
                            pool.wait_ge(S["tc_ready"], b)
                        r0, i0 = reim[:, :, 0:1], reim[:, :, 1:2]
                    step(pool.tensor_tensor(r0, t[0], t[1], ALU.subtract))
                    step(pool.tensor_tensor(i0, t[2], t[3], ALU.add), last)
                    w //= 2
                r, i = reim[:, :, 0], reim[:, :, 1]
                u, v, w_, x_ = (st[:, j, :] for j in range(4))
                if first(b):
                    pool.wait_ge(S["gram_sb"], 1)
                step(pool.tensor_scalar(u, r, gram[:, 0:1], gram[:, 5:6], ALU.mult, ALU.add), True)
                step(pool.tensor_scalar(w_, i, gram[:, 3:4], 0.0, ALU.mult, ALU.add))
                step(pool.tensor_tensor(u, u, w_, ALU.add))
                step(pool.tensor_tensor(u, u, r, ALU.mult), True)
                step(pool.tensor_scalar(v, i, gram[:, 1:2], gram[:, 4:5], ALU.mult, ALU.add))
                step(pool.tensor_tensor(v, v, i, ALU.mult))
                step(pool.tensor_tensor(u, u, v, ALU.add))
                if not first(b):
                    pool.wait_ge(S["sd_ready"], 2 * b)
                waiting()
                pool.tensor_scalar(x_, u, gram[:, 2:3], 0.0, ALU.add, ALU.max).then_inc(S["var_ready"], 1)
                assert count[0] == POOL_STEPS, count[0]

            def spread(b, k):
                c = C9 * b + k
                pool.wait_ge(S["rd_ready"], c + 1)
                pool.wait_ge(S["rdt_ps"], past(2 * c))
                waiting()
                pool.tensor_scalar(rd_all[:, :, :, :],
                                   rd[:, :, :].rearrange("p n (h o) -> p n h o", o=1).to_broadcast([P, 4, H, DH]),
                                   1.0, 0.0, ALU.mult, ALU.add).then_inc(S["rdb_ready"], 1)

            def batch(b, last):
                if not last:
                    tokens(b + 1)
                if last:
                    pool.wait_ge(S["z_ready"], NB)
                    for half in range(2):
                        pool.memset(w1b_z[64 - 64 * half:128 - 64 * half, half:E:2, :], 0.0).then_inc(S["f_zero"], 1)
                        pool.wait_ge(S["f_zero"], half + 1)
                with pool.Fori(0, C9) as k:
                    spread(b, k)

            pool.wait_ge(s_const, 16)
            tokens(0)
            with pool.Fori(0, NB - 1) as b:
                batch(b, False)
            batch(NB - 1, True)

        @block.scalar
        def _(act):
            def sines(b):
                act.wait_ge(S["ang_ready"], 2 * b + 1)
                if not first(b):
                    act.wait_ge(S["var_ready"], b)
                act.activation(sin_a[:, :, :], ang[0][:, :, :], ACT.Sin, scale=0.5).then_inc(S["sin_ready"], 1)
                act.activation(abs_a[:, :, :], ang[0][:, :, :], ACT.Abs, scale=0.5).then_inc(S["sin_ready"], 1)
                act.wait_ge(S["sin_ready"], 4 * b + 2)
                act.activation(re[:, :, :], abs_a[:, :, :], ACT.Sin, bias=halfpi[:, :], scale=-1.0).then_inc(
                    S["sin_ready"], 1)
                act.wait_ge(S["ang_ready"], 2 * b + 2)
                act.activation(im[:, :, :], ang[1][:, :, :], ACT.Sin, scale=2.0).then_inc(S["sin_ready"], 1)

            def deviations(b):
                act.wait_ge(S["var_ready"], b + 1)
                act.activation(sd[:, :], st[:, 3, :], ACT.Sqrt, bias=eps_col[:, :]).then_inc(S["sd_ready"], 1)
                act.wait_ge(S["txvar_ready"], b + 1)
                act.activation(txsd[:, 0:1], txmv[:, 1:2], ACT.Sqrt, bias=eps_col[:, :]).then_inc(S["sd_ready"], 1)

            def setup_sequence(b):
                for i in range(5):
                    act.wait_ge(S["coef_ps"], C9 * b + 2 * i + 1)
                    w = 512 if i < 4 else P
                    act.activation(coef_t[:, 1024 * i:1024 * i + w], psb(0)[:, 0:w], ACT.Copy).then_inc(
                        S["coef_act"], 1)
                act.wait_ge(S["qkx_ps"], b + 1)
                act.activation(qkv_x[:, 0:512], ps[:, 3, :], ACT.Copy).then_inc(S["qkx_sb"], 1)
                act.activation(qkv_x[:, 512:768], ps[:, 4, 0:256], ACT.Copy).then_inc(S["qkx_sb"], 1)
                for i, (g, bank, half) in enumerate(G_ORDER):
                    act.wait_ge(S["g_ps"], 4 * b + i + 1)
                    for r in (slice(0, 32), slice(64, 128)):
                        ins = act.activation(g[r, 512 * half:512 * half + 512], ps[r, bank, :], ACT.Copy)
                    ins.then_inc(S["g_first"], 1)
                    if i == 0:
                        act.wait_ge(S["s2_sub"], b + 1)
                        act.activation(s2[:, :, :], s2[:, :, :], ACT.Exp).then_inc(S["s2_exp"], 1)
                for i in range(2):
                    act.wait_ge(S["xt_ps"], 2 * b + i + 1)
                    act.activation(xt[:, 4 * i:4 * i + 4, :], ps[:, i, :].rearrange("p (n c) -> p n c", n=4),
                                   ACT.Copy).then_inc(S["xt_sb"], 1)

            def pseudo_inverse(b):
                pe, done = [0, 0], [0, 0]
                for s, k, half, _ in pinv_steps():
                    rows = slice(4 * half, 4 * half + 4)

                    def bank(i):
                        return ps[:, 3 * half + i, :].rearrange("p (n c) -> p n c", n=4)

                    def copy(dst, i, scale):
                        act.activation(dst[:, rows, :], bank(i), ACT.Copy, scale=scale).then_inc(
                            S[f"pi_act{half}"], 1)
                        done[half] += 1

                    pe[half] += 1
                    act.wait_ge(S[f"pi_pe{half}"], PI_PE * b + pe[half])
                    if s == "init":
                        copy(ym, 0, 1.0)
                        copy(yt, 1, 1.0)
                    elif s == "square":
                        copy(y2t, 0, 1.0)
                    elif s == "next" and k < ITERS - 1:
                        copy(ym, 0, 0.25)
                        copy(yt, 1, 0.25)
                        copy(vt, 2, 0.25)
                    elif s == "next":
                        copy(vt, 2, 0.25)
                assert done[0] == PI_ACT and pe[0] == PI_PE

            def exp3(b, n, j):
                act.wait_ge(S["s3_pe"], TILES * b + n + 1)
                act.activation(p3[:, j, :], ps[:, 2 * (j % 2):2 * (j % 2) + 2, :].rearrange("p a c -> p (a c)"),
                               ACT.Exp).then_inc(S["s3_exp"], 1)

            def landmark_probs(b):
                if not first(b):
                    act.wait_ge(S["ud_pe"], past(2 * C9 * b))
                for j in range(4):
                    exp3(b, j, j)

                def more(k):
                    for j in range(4):
                        if j % 2 == 0:
                            act.wait_ge(S["pv3_pe"], 17 * b + 2 * k + j // 2 - 1)
                        exp3(b, 4 * k + j, j)

                with act.Fori(1, CH) as k:
                    more(k)
                act.wait_ge(S["pv3_pe"], 17 * b + 15)
                exp3(b, NT, 0)

            def group(b, k, g, pp, w):
                c = C9 * b + k
                if pp == 0:
                    if first(k):
                        act.wait_ge(S["o3_ps"], b + 1)
                    elif not first(c):
                        act.wait_ge(S["ud_pe"], past(2 * c + g - 1))
                act.wait_ge(S["s1_pe"], 8 * c + 4 * g + pp + 1)
                act.activation(p1[:, g, pp, 0:w], ps[:, 2 + pp % 2, 0:w], ACT.Exp).then_inc(S["p1_ready"], 1)

            def u_copy(b, k, g, par, w):
                c = C9 * b + k
                act.wait_ge(S["ud_pe"], past(2 * c + g + 1))
                act.activation(u_sb[:, par, g, 0:w], ps[:, 4, 0:w], ACT.Copy).then_inc(S["u_ready"], 1)

            def out_copy(b, kp, par):
                cp = C9 * b + kp
                act.wait_ge(S["out_ps"], past(2 * cp + 2))
                act.activation(out_sb[:, par, 2:4, :], ps[:, 6, :].rearrange("p (n c) -> p n c", n=2),
                               ACT.Copy).then_inc(S["out_ready"], 1)

            def chunk(b, k, par, w, before):
                for pp in range(4):
                    group(b, k, 0, pp, w)
                group(b, k, 1, 0, w)
                u_copy(b, k, 0, par, w)
                if before:
                    out_copy(b, k - 2, par)
                for pp in range(1, 4):
                    group(b, k, 1, pp, w)
                u_copy(b, k, 1, par, w)

            def batch(b, last):
                setup_sequence(b)
                if not last:
                    sines(b + 1)
                pseudo_inverse(b)
                landmark_probs(b)
                if not last:
                    deviations(b + 1)
                chunk(b, 0, 0, 512, False)
                chunk(b, 1, 1, 512, False)
                with act.Fori(1, CH // 2 - 1) as i:
                    chunk(b, 2 * i, 0, 512, True)
                    chunk(b, 2 * i + 1, 1, 512, True)
                chunk(b, CH - 2, 0, 512, True)
                chunk(b, CH - 1, 1, 512, True)
                chunk(b, CH, 0, P, True)
                out_copy(b, CH - 1, 1)

            act.wait_ge(s_zero, 14)
            sines(0)
            deviations(0)
            with act.Fori(0, NB - 1) as b:
                batch(b, False)
            batch(NB - 1, True)

            act.wait_ge(S["f_var"], 1)
            act.activation(fsd[:, 0, :], fmv[:, :, 1], ACT.Sqrt, bias=eps_col[:, :]).then_inc(S["f_sd"], 1)
            with act.Fori(0, FT // 4) as c:
                for p in range(E // 2):
                    for f in range(FB):
                        u = (4 * c + p) * FB + f
                        for e in range(2):
                            act.wait_ge(S["f_l1"], 2 * u + e + 1)
                            act.activation(hid[:, e, f % 2, :], ps[:, 2 * (f % 2) + e, :], ACT.Gelu).then_inc(
                                S["f_gelu"], 1)

        @block.vector
        def _(dve):
            count = [0]
            base = [0]

            def step(ins):
                count[0] += 1
                ins.then_inc(dve_step, 1)
                dve.wait_ge(dve_step, base[0] + count[0])

            def split(dst, src, width):
                r = split_r[64:128, 0:width]
                dve.tensor_copy(dst[0:32], src[0:32])
                step(dve.tensor_copy(dst[64:128], src[64:128]))
                return lower_parts(dst, src, width)

            def lower_parts(dst, src, width):
                r = split_r[64:128, 0:width]
                step(dve.tensor_tensor(r, src[64:128], dst[64:128], ALU.subtract))
                step(dve.tensor_copy(dst[64:128], r))
                return dve.tensor_tensor(dst[96:128], split_r[96:128, 0:width], dst[96:128], ALU.subtract)

            def split_g(b, i):
                g, bank, half = G_ORDER[i]
                dve.wait_ge(S["g_first"], 4 * b + i + 1)
                if i:
                    dve.wait_ge(S["g_ready"], 4 * b + i)
                lower_parts(g[:, 512 * half:512 * half + 512], ps[:, bank, :], 512).then_inc(S["g_ready"], 1)

            for i, name in enumerate(FROM_ONE):
                dve.memset(started[:, i:i + 1], 0.0).then_inc(S[name], 1)

            dve.wait_ge(s_const, 16)
            dve.wait_ge(s_w, 16 * 7)
            dve.wait_ge(s_zero, 14)
            dve.tensor_copy(identb[:, :], ident)
            dve.tensor_copy(g1[32:64, :], con("negind")[32:64])
            dve.tensor_scalar(id7[:, :], ident, 7.0, None, ALU.mult)
            dve.tensor_scalar(id13[:, :], ident, 13.0, None, ALU.mult)
            dve.tensor_scalar(wq[:, :, 0:D], wq[:, :, 0:D], DH ** -0.5, None, ALU.mult)
            dve.tensor_scalar(bq[:, 0:D], bq[:, 0:D], DH ** -0.5, None, ALU.mult)
            step(dve.tensor_reduce(ksum[:, 0:1], kb[:, :], AX.X, ALU.add))
            step(dve.tensor_scalar(ksum[:, 1:2], ksum[:, 0:1], 1.0 / D, None, ALU.mult))
            dve.tensor_scalar(kbc[:, :], kb[:, :], ksum[:, 1:2], None, ALU.subtract).then_inc(S["kbc_ready"], 1)
            dve.wait_ge(S["kt_ps"], 1)
            step(dve.tensor_copy(kt4[:, :, 0:3], ps[:, 0, 0:8].rearrange("p (k c) -> p k c", k=2)[:, :, 0:3]))
            dve.tensor_tensor(prod[:, :, 0:3], kt4[:, :, 0:3], kt4[:, :, 0:3], ALU.mult)
            dve.tensor_tensor(prod[:, :, 3:5], kt4[:, :, 0:2], kt4[:, :, 1:3], ALU.mult)
            dve.tensor_tensor(prod[:, :, 5:6], kt4[:, :, 0:1], kt4[:, :, 2:3], ALU.mult).then_inc(S["kt4_ready"], 1)
            dve.wait_ge(S["gram_ps"], 1)
            dve.tensor_copy(gram[:, 0:3], ps[:, 1, 0:3])
            dve.tensor_scalar(gram[:, 3:6], ps[:, 1, 3:6], 2.0, None, ALU.mult).then_inc(S["gram_sb"], 1)
            dve.wait_ge(S["m4_ps"], 1)
            dve.tensor_copy(m4[:, 0:512], ps[0:4, 2, :])
            dve.tensor_copy(m4[:, 512:768], ps[0:4, 3, 0:256]).then_inc(S["m4_sb"], 1)
            dve.wait_ge(S["mt_ps"], 1)
            for n in (1, 2, 3):
                for col in A_COLS[n]:
                    dve.tensor_copy(mt[:, :, col:col + 4], ps[:, 4, 0:16].rearrange("p (n c) -> p n c", n=4))
            dve.wait_ge(S["v4_ps"], 1)
            for half in range(2):
                dve.tensor_copy(v4x[:, 4 * half:4 * half + 4, 0:32],
                                ps[:, 5, 128 * half:128 * half + 128].rearrange("p (n c) -> p n c", n=4))
                dve.tensor_copy(v4x[:, 4 * half:4 * half + 4, 32:33],
                                con("col32")[:, half:half + 1].rearrange("p (a b) -> p a b", a=1).to_broadcast([P, 4, 1]))
            dve.wait_ge(S["bout_ps"], 1)
            dve.tensor_copy(bout_all[:, :], ps[:, 7, 0:256])
            dve.memset(res_w[32:64, :], 0.0)
            split(res_w, ps[:, 6, 0:256], D).then_inc(S["setup_sb"], 1)
            SETUP = count[0]
            PER = 23

            def text_stats(b):
                dve.wait_ge(s_txin, 16 * b + 16)
                step(dve.bn_stats(txstat[:, :], tx[:, :]))

            def text_variance():
                dve.bn_aggr(txmv[:, :], txstat[:, :]).then_inc(S["txvar_ready"], 1)

            def setup_sequence(b):
                dve.wait_ge(S["sd_ready"], 2 * b + 2)
                step(dve.reciprocal(txsd[:, 1:2], txsd[:, 0:1]))
                dve.tensor_scalar(txn[:, :], tx[:, :], txmv[:, 0:1], txsd[:, 1:2], ALU.subtract, ALU.mult).then_inc(
                    S["txn_ready"], 1)
                dve.tensor_tensor(txr[:, :], tx[:, :], bout_all[:, :], ALU.add).then_inc(S["tx_used"], 1)
                step(dve.reciprocal(rstd[:, :], sd[:, :]))
                rb = rstd[:, :].rearrange("p (n o) -> p n o", o=1)
                dve.tensor_copy(cf[:, 0:NT, 2:3], rb)
                step(dve.tensor_tensor(cf[:, 0:NT, 0:2], reim[:, :, :], rb.to_broadcast([P, NT, 2]), ALU.mult))

                def parts(src, tmp, n, cols):
                    t = tc[:, 0:NT, :]
                    for c in cols[1][1:]:
                        dve.tensor_copy(t[:, :, c:c + n], src)
                    c = cols[1][0]
                    step(dve.tensor_copy(t[:, :, c:c + n], src))
                    step(dve.tensor_tensor(tmp, src, t[:, :, c:c + n], ALU.subtract))
                    for c in cols[2][1:]:
                        dve.tensor_copy(t[:, :, c:c + n], tmp)
                    c = cols[2][0]
                    step(dve.tensor_copy(t[:, :, c:c + n], tmp))
                    c3_ = cols[3][0]
                    return dve.tensor_tensor(t[:, :, c3_:c3_ + n], tmp, t[:, :, c:c + n], ALU.subtract)

                step(parts(cf[:, 0:NT, 0:4], ce[:, :, :], 4, A_COLS))
                parts(reim[:, :, :], ce[:, :, 0:2], 2, B_COLS).then_inc(S["tc_ready"], 1)
                dve.memset(g3[32:64, :], 0.0)
                dve.wait_ge(S["txnt_ps"], b + 1)
                dve.tensor_copy(txn_t[:, :, :], ps[:, 2, 0:256].rearrange("p (k c) -> p k c", k=2)).then_inc(
                    S["txnt_sb"], 1)
                for i in range(4):
                    dve.wait_ge(S["coef_ps"], C9 * b + 2 * i + 2)
                    dve.tensor_copy(coef_t[:, 1024 * i + 512:1024 * i + 1024], psb(1)[:, 0:512]).then_inc(
                        S["coef_dve"], 1)
                dve.wait_ge(S["lm_ps"], b + 1)
                dve.tensor_copy(lm_c[:, :], ps[0:4, 6, 0:LM]).then_inc(S["lm_sb"], 1)
                dve.wait_ge(S["qkxt_ps"], b + 1)
                dve.tensor_copy(qk_xt[:, :, :], ps[:, 5, :].rearrange("p (n c) -> p n c", n=4)).then_inc(
                    S["qkxt_sb"], 1)
                dve.wait_ge(S["qkl_ps"], b + 1)
                qkl = ps[:, 7, 0:256].rearrange("p (n o j) -> p n o j", n=4, o=1)
                mask = con("mask8").rearrange("p (h o) -> p h o", o=1).to_broadcast([P, 8, LM])
                for t, part in ((kl_bd, 2), (ql_bd, 0)):
                    for half in range(2):
                        ins = dve.tensor_tensor(t[:, half, :, :], qkl[:, part + half, :, :].to_broadcast([P, 8, LM]),
                                                mask, ALU.mult)
                    if part == 2:
                        dve.tensor_copy(klt[:, :, :], qkl[:, 2:4, 0, :]).then_inc(S["klbd_ready"], 1)
                    else:
                        ins.then_inc(S["qlbd_ready"], 1)
                dve.wait_ge(S["s2_ps"], b + 1)
                s2_ps = ps[:, 4, :].rearrange("p (n c) -> p n c", n=PAIRS)
                step(dve.tensor_reduce(s2m[:, 0, :], s2_ps, AX.X, ALU.max))
                dve.tensor_tensor(s2[:, :, :], s2_ps,
                                  s2m[:, 0, :].rearrange("p (n o) -> p n o", o=1).to_broadcast([P, PAIRS, LM]),
                                  ALU.subtract).then_inc(S["s2_sub"], 1)
                split_g(b, 0)
                dve.wait_ge(S["s2_exp"], b + 1)
                step(dve.tensor_reduce(s2m[:, 0, :], s2[:, :, :], AX.X, ALU.add))
                step(dve.reciprocal(s2m[:, 1, :], s2m[:, 0, :]))
                for i in range(2):
                    r = slice(64 * i, 64 * i + 64)
                    ins = dve.tensor_tensor(
                        xbd[r, :, 64 * i:64 * i + 64], s2[r, :, :],
                        s2m[r, 1, :].rearrange("p (n o) -> p n o", o=1).to_broadcast([64, PAIRS, LM]), ALU.mult)
                ins.then_inc(S["xbd_ready"], 1)
                for i in range(1, 4):
                    split_g(b, i)

            def pseudo_inverse(b):
                pe, act_n, units = [0, 0], [0, 0], [0]
                for s, k, half, fill in pinv_steps():
                    rows = slice(4 * half, 4 * half + 4)

                    def bank(i):
                        return ps[:, 3 * half + i, :].rearrange("p (n c) -> p n c", n=4)

                    def eye(t):
                        return t[:, :].rearrange("p (o c) -> p o c", o=1).to_broadcast([P, 4, P])

                    pe[half] += 1
                    if s == "init" or (s == "next" and k < ITERS - 1):
                        dve.wait_ge(S[f"pi_act{half}"], past(PI_ACT * b + act_n[half] + 1))
                        act_n[half] += 2 if s == "init" else 3
                        dve.scalar_tensor_tensor(out=y7[:, rows, :], in0=ym[:, rows, :], scalar=-1.0, in1=eye(id7),
                                                 op0=ALU.mult, op1=ALU.add)
                        dve.scalar_tensor_tensor(out=ylin[:, rows, :], in0=ym[:, rows, :], scalar=-15.0,
                                                 in1=eye(id13), op0=ALU.mult, op1=ALU.add).then_inc(
                            S[f"pi_dve{half}"], 1)
                    elif s == "square":
                        act_n[half] += 1
                    elif s == "poly":
                        dve.wait_ge(S[f"pi_pe{half}"], PI_PE * b + pe[half])
                        dve.wait_ge(S[f"pi_dve{half}"], past(PI_DVE * b + 2 * k + 1))
                        dve.tensor_tensor(qm[:, rows, :], bank(1), ylin[:, rows, :], ALU.add).then_inc(
                            S[f"pi_dve{half}"], 1)
                    for p, d in fill:
                        units[0] += 1
                        dve.wait_ge(S["s3m_pe"], len(score_units()) * b + units[0])
                        if p is None:
                            dve.tensor_reduce(m3part[:, :, d], ps[:, 6:8, :].rearrange("p a (n c) -> p (a n) c", n=4),
                                              AX.X, ALU.max).then_inc(S["s3m_used"], 1)
                        else:
                            dve.tensor_reduce(m3part[:, p, d:d + 1], ps[:, 6:8, :].rearrange("p a c -> p (a c)"),
                                              AX.X, ALU.max).then_inc(S["s3m_used"], 1)
                dve.wait_ge(S["s3m_used"], past(len(score_units()) * (b + 1)))
                dve.tensor_reduce(m3z[:, :, 16:17], m3part[:, :, :], AX.X, ALU.max).then_inc(S["m3_ready"], 1)
                dve.wait_ge(S["m3_ps"], b + 1)
                dve.tensor_scalar(g3[32:64, :], ps[32:64, 6:8, :].rearrange("p a c -> p (a c)"), -1.0, None,
                                  ALU.mult).then_inc(S["g3_shift"], 1)

            def weights(b, k, half):
                if not (isinstance(k, int) and k < 2):
                    dve.wait_ge(S["pv3_pe"], 17 * b + 2 * k - 2)
                dve.tensor_copy(cfw[:, 4 * half:4 * half + 4, :], cf[:, ds(4 * k, 4), :]).then_inc(S["cfw_ready"], 1)

            def landmark_values(b):
                for k in range(2):
                    weights(b, k, k)
                with dve.Fori(1, CH // 2) as i:
                    weights(b, 2 * i, 0)
                    weights(b, 2 * i + 1, 1)
                dve.wait_ge(S["pv3_pe"], 17 * (b + 1))
                dve.tensor_copy(c3[:, :], ps[:, 4, :]).then_inc(S["c3_sb"], 1)
                dve.wait_ge(S["o3_ps"], b + 1)
                o3 = ps[:, 5, 0:272].rearrange("p (n c) -> p n c", n=PAIRS)
                step(dve.reciprocal(w3r[:, :], o3[:, :, 32]))
                for i in range(2):
                    r = slice(64 * i, 64 * i + 64)
                    ins = dve.tensor_tensor(
                        w3[r, :, :], o3[r, :, 16 * i:16 * i + 16],
                        w3r[r, :].rearrange("p (n o) -> p n o", o=1).to_broadcast([64, PAIRS, DH]), ALU.mult)
                ins.then_inc(S["w3_ready"], 1)
                dve.wait_ge(S["z_ps"], b + 1)
                for i in range(2):
                    r = slice(64 * i, 64 * i + 64)
                    ins = dve.tensor_copy(z_bd[r, :, 16 * i:16 * i + 16],
                                          ps[r, 6, 0:128].rearrange("p (n c) -> p n c", n=PAIRS))
                ins.then_inc(S["z_ready"], 1)

            def row_max(b, k, j, text):
                t = 4 * (C9 * b + k) + j
                dve.wait_ge(S["s1m_pe"], t + 1)
                dve.tensor_reduce(m1[:, j, :], ps[:, 0:2, :].rearrange("p a (h c) -> p (a h) c", c=LM), AX.X,
                                  ALU.max).then_inc(S["s1m_used"], 4 if text else 1)

            def max_rows(b, k, w):
                dve.wait_ge(S["m1t_ps"], C9 * b + k + 1)
                dve.tensor_copy(coef_t[MAXROW:MAXROW + H, ds(512 * k, w)], psb(0)[MAXROW:MAXROW + H, 0:w]).then_inc(
                    S["m1t_sb"], 1)

            def denominators(b, kp, w):
                cp = C9 * b + kp
                n = w // P
                dve.wait_ge(S["dt_ps"], past(cp + 1))
                dve.tensor_reduce(d_t[:, 0:n, :], ps[:, 7, 0:w].rearrange("p (n q h) -> p n h q", n=n, q=4)[:, :, 0:H, :],
                                  AX.X, ALU.add).then_inc(S["dt_used"], 1)
                dve.wait_ge(S["dt_used"], cp + 1)
                if not first(cp):
                    dve.wait_ge(S["rdb_ready"], past(cp))
                dve.reciprocal(rd[:, 0:n, :], d_t[:, 0:n, :]).then_inc(S["rd_ready"], 1)

            def normalise(b, kp, g, par, w):
                cp = C9 * b + kp
                dve.wait_ge(S["rdt_ps"], past(2 * cp + g + 1))
                dve.wait_ge(S["u_ready"], past(2 * cp + g + 1))
                if g == 0:
                    dve.wait_ge(S["out_ps"], past(2 * cp))
                dve.tensor_tensor(o_sb[:, g, 0:w], ps[:, 7, 0:w], u_sb[:, par, g, 0:w], ALU.mult).then_inc(
                    S["o_ready"], 1)

            def d_copy(b, k, w):
                dve.wait_ge(S["ud_pe"], past(2 * (C9 * b + k) + 2))
                dve.wait_ge(S["dt_ps"], past(C9 * b + k))
                dve.tensor_copy(d_sb[:, 0:w], ps[:, 5, 0:w]).then_inc(S["d_ready"], 1)

            def out_copy(b, kp, par, i):
                dve.wait_ge(S["out_ps"], past(2 * (C9 * b + kp) + 1))
                dve.wait_ge(S[f"out_stored{par}"], past(16 * ((5 - par) * b + i)))
                dve.tensor_copy(out_sb[:, par, 0:2, :], ps[:, 6, :].rearrange("p (n c) -> p n c", n=2)).then_inc(
                    S["out_ready"], 1)

            def text_out(b):
                cp = C9 * b + CH
                dve.wait_ge(S["out_ps"], past(2 * cp + 1))
                dve.wait_ge(S["out_stored0"], past(16 * (5 * b + 4)))
                dve.tensor_tensor(out_sb[:, 0, 0, :], ps[:, 6, 0:256], txr[:, :], ALU.add).then_inc(S["out_ready"], 2)

            def chunk(b, k, par, w, prev, nxt, i=0):
                text_next = nxt and isinstance(k, int) and k == CH - 1
                rows = nxt and not text_next
                if prev:
                    denominators(b, k - 1, 512)
                if nxt:
                    row_max(b, k + 1, 0, text_next)
                if prev:
                    normalise(b, k - 1, 0, 1 - par, 512)
                if rows:
                    row_max(b, k + 1, 1, False)
                if prev:
                    normalise(b, k - 1, 1, 1 - par, 512)
                if rows:
                    row_max(b, k + 1, 2, False)
                    row_max(b, k + 1, 3, False)
                d_copy(b, k, w)
                if nxt:
                    max_rows(b, k + 1, P if text_next else 512)
                if prev:
                    out_copy(b, k - 1, 1 - par, i)

            def batch(b, last):
                count[0] = 0
                base[0] = SETUP + 1 + PER * b
                setup_sequence(b)
                pseudo_inverse(b)
                landmark_values(b)
                if not last:
                    text_stats(b + 1)
                else:
                    count[0] += 1
                row_max(b, 0, 0, False)
                if not last:
                    text_variance()
                for j in range(1, 4):
                    row_max(b, 0, j, False)
                max_rows(b, 0, 512)
                chunk(b, 0, 0, 512, False, True)
                chunk(b, 1, 1, 512, True, True, 0)
                with dve.Fori(1, CH // 2 - 1) as i:
                    chunk(b, 2 * i, 0, 512, True, True, i - 1)
                    chunk(b, 2 * i + 1, 1, 512, True, True, i)
                chunk(b, CH - 2, 0, 512, True, True, 2)
                chunk(b, CH - 1, 1, 512, True, True, 3)
                chunk(b, CH, 0, P, True, False, 3)
                denominators(b, CH, P)
                normalise(b, CH, 0, 0, P)
                normalise(b, CH, 1, 0, P)
                text_out(b)
                assert count[0] == PER, count[0]

            text_stats(0)
            text_variance()
            with dve.Fori(0, NB - 1) as b:
                batch(b, False)
            batch(NB - 1, True)

            base[0] = SETUP + PER * NB
            count[0] = 0
            dve.wait_ge(S["f_e"], 32)
            step(dve.tensor_copy(ei_f[:, :, :], ei_s[:, :, :]))
            for k in range(2):
                iota = con("iota8").rearrange("p (o e) -> p o e", o=1).to_broadcast([P, FT, E])
                step(dve.tensor_tensor(eq[:, k, :, :], ei_f[:, :, k:k + 1].to_broadcast([P, FT, E]), iota, ALU.is_equal))
                step(dve.tensor_tensor(eq[:, k, :, :], eq[:, k, :, :], ew_s[:, :, k:k + 1].to_broadcast([P, FT, E]),
                                       ALU.mult))
            dve.tensor_tensor(eq[:, 0, :, :], eq[:, 0, :, :], eq[:, 1, :, :], ALU.add).then_inc(S["f_we"], 1)
            dve.wait_ge(S["f_x"], 16)
            for n in range(FT):
                ins = dve.bn_stats(fst[:, n, :], x1[:, n, :])
            step(ins)
            for n in range(FT):
                ins = dve.bn_aggr(fmv[:, n, :], fst[:, n, :])
            ins.then_inc(S["f_var"], 1)
            dve.wait_ge(S["f_sd"], 1)
            step(dve.reciprocal(fsd[:, 1, :], fsd[:, 0, :]))

            def normalise_rows(c):
                if not first(c):
                    dve.wait_ge(S["f_xnt_ps"], 2 * c)
                for j in range(4):
                    ins = dve.tensor_scalar(xn[:, j, :], x1[:, ds(4 * c + j, 1), :].rearrange("p o c -> p (o c)"),
                                            fmv[:, ds(4 * c + j, 1), 0:1].rearrange("p a b -> p (a b)"),
                                            fsd[:, 1, ds(4 * c + j, 1)], ALU.subtract, ALU.mult)
                ins.then_inc(S["f_xn"], 1)

            def turned_rows(c):
                for i in range(2):
                    dve.wait_ge(S["f_xnt_ps"], 2 * c + i + 1)
                    dve.tensor_copy(xn_t[:, :, 256 * i:256 * i + 256],
                                    ps[:, 6 + i, :].rearrange("p (k c) -> p k c", k=2)).then_inc(S["f_xnt"], 1)

            def out_rows(c):
                for i in range(2):
                    dve.wait_ge(S["f_out_ps"], 2 * c + i + 1)
                    if i == 0:
                        dve.wait_ge(S["f_stored"], past(16 * c))
                    dve.tensor_tensor(out_sb[:, 0, 2 * i:2 * i + 2, :], ps[:, 6 + i, :].rearrange("p (n c) -> p n c", n=2),
                                      x1[:, ds(4 * c + 2 * i, 2), :], ALU.add).then_inc(S["f_out"], 1)

            def experts(c, last):
                for p in range(E // 2):
                    dve.wait_ge(S["f_l0"], 4 * c + p + 1)
                    dve.tensor_copy(mid[:, p, :], ps[:, 4 + p % 2, :]).then_inc(S["f_mid"], 1)
                if not first(c):
                    out_rows(c - 1)
                for p in range(E // 2):
                    if p == 1 and not last:
                        normalise_rows(c + 1)
                    dve.wait_ge(S["f_wx_ps"], 4 * c + p + 1)
                    if not (first(c) and p == 0):
                        dve.wait_ge(S["f_y2"], 4 * c + p)
                    dve.tensor_copy(wx[:, :], ps[:, 6, :]).then_inc(S["f_wx"], 1)
                    if p == 2 and not last:
                        turned_rows(c + 1)
                    dve.wait_ge(S["f_wx"], 4 * c + p + 1)
                    dve.wait_ge(S["f_l2"], FB * (4 * c + p + 1))
                    dve.tensor_tensor(y2[:, p, :], ps[:, 4 + p % 2, :], wx[:, :], ALU.mult).then_inc(S["f_y2"], 1)

            normalise_rows(0)
            dve.wait_ge(S["out_stored0"], past(16 * 5 * NB))
            step(dve.memset(we_t[:, :], 0.0))
            for i in range(4):
                dve.wait_ge(S["f_wet_ps"], i + 1)
                dve.tensor_copy(we_t[0:E, 512 * i:512 * i + 512], ps[0:E, i, :]).then_inc(S["f_wet"], 1)
            turned_rows(0)
            experts(0, False)
            with dve.Fori(1, FT // 4 - 1) as c:
                experts(c, False)
            experts(FT // 4 - 1, True)
            out_rows(FT // 4 - 1)

        @block.tensor
        def _(pe):
            pe.wait_ge(S["kbc_ready"], 1)
            for k in range(2):
                ins = pe.transpose(ps[:, 0, 4 * k:4 * k + 3], kbc[:, 128 * k:128 * k + 128], ident[0:3, 0:3])
            ins.then_inc(S["kt_ps"], 1)
            pe.wait_ge(S["kt4_ready"], 1)
            for k in range(2):
                ins = pe.matmul(ps[:, 1, 0:6], mean_w[:, :], prod[:, k, :], start=k == 0, stop=k == 1)
            ins.then_inc(S["gram_ps"], 1)
            e3 = con("e3")[0:1, :]
            for i, (a, n) in enumerate(((0, 512), (512, 256))):
                for k in range(2):
                    pe.matmul(ps[0:4, 2 + i, 0:n], kt4[:, k, :], wq[:, k, a:a + n], start=k == 0, stop=False)
                ins = pe.matmul(ps[0:4, 2 + i, 0:n], e3, bq[:, a:a + n], start=False, stop=True)
            ins.then_inc(S["m4_ps"], 1)
            for n in range(4):
                o = ps[:, 4, 4 * n:4 * n + 4]
                for k in range(2):
                    pe.matmul(o, wq[:, k, 128 * n:128 * n + 128], kt4[:, k, :], start=k == 0, stop=False)
                ins = pe.matmul(o, bq[:, 128 * n:128 * n + 128], e3, start=False, stop=True)
            ins.then_inc(S["mt_ps"], 1)
            pe.wait_ge(S["m4_sb"], 1)
            for half in range(2):
                ins = pe.matmul(ps[:, 5, 128 * half:128 * half + 128],
                                con("selV")[0:4, 128 * half:128 * half + 128],
                                m4[:, 512 + 128 * half:640 + 128 * half], start=True, stop=True)
            ins.then_inc(S["v4_ps"], 1)
            pe.matmul(ps[:, 6, 0:256], con("sel3")[0:3, :], kb[:, :], start=True, stop=False)
            pe.matmul(ps[:, 6, 0:256], con("sel1")[0:1, :], bo[:, :], start=False, stop=True)
            pe.matmul(ps[:, 7, 0:256], ones_row[:, :], bo[:, :], start=True, stop=True).then_inc(S["bout_ps"], 1)
            pe.wait_ge(S["setup_sb"], 1)

            def setup_sequence(b):
                pe.wait_ge(S["txn_ready"], b + 1)
                for k in range(2):
                    ins = pe.transpose(ps[:, 2, 128 * k:128 * k + 128], txn[:, 128 * k:128 * k + 128], ident)
                ins.then_inc(S["txnt_ps"], 1)
                pe.wait_ge(S["tc_ready"], b + 1)

                def text_qkv():
                    pe.wait_ge(S["txnt_sb"], b + 1)
                    for i, (a, n) in enumerate(((0, 512), (512, 256))):
                        for k in range(2):
                            ins = pe.matmul(ps[:, 3 + i, 0:n], txn_t[:, k, :], wq[:, k, a:a + n], start=k == 0,
                                            stop=i == 1 and k == 1)
                        if i == 0:
                            pe.matmul(ps[:, 3, :], ones_row[:, :], bq[:, 0:512], start=False, stop=True)
                    ins.then_inc(S["qkx_ps"], 1)

                for i in range(C9):
                    if i == 2:
                        text_qkv()
                    if i >= 2:
                        pe.wait_ge(S["coef_dve"], 4 * b + i // 2) if i % 2 else pe.wait_ge(S["coef_act"], 5 * b + i // 2)
                    for j in range(4 if i < CH else 1):
                        ins = pe.transpose(psb(i % 2)[:, 128 * j:128 * j + 128], tc[:, 4 * i + j, :], identb[:, :])
                    ins.then_inc(S["coef_ps"], 1)
                for n in range(NT):
                    ins = pe.matmul(ps[0:32, 6, 0:LM], cf[:, n, :], sb_member[:, n, :], start=n == 0, stop=n == NT - 1)
                ins.then_inc(S["lm_ps"], 1)
                pe.wait_ge(S["qkx_sb"], 2 * b + 2)
                for n in range(4):
                    ins = pe.transpose(ps[:, 5, 128 * n:128 * n + 128], qkv_x[:, 128 * n:128 * n + 128], ident)
                ins.then_inc(S["qkxt_ps"], 1)
                pe.wait_ge(S["lm_sb"], b + 1)
                for n in range(4):
                    o = ps[:, 7, LM * n:LM * n + LM]
                    pe.matmul(o, m4[:, 128 * n:128 * n + 128], lm_c[:, :], start=True, stop=False)
                    ins = pe.matmul(o, qkv_x[:, 128 * n:128 * n + 128], sb_member[:, NT, :], start=False, stop=True)
                ins.then_inc(S["qkl_ps"], 1)
                pe.wait_ge(S["klbd_ready"], b + 1)
                pe.wait_ge(S["qlbd_ready"], b + 1)
                pe.wait_ge(S["qkxt_sb"], b + 1)
                for p in range(PAIRS):
                    half, q = p // 4, 2 * (p % 4)
                    ins = pe.matmul(ps[:, 4, LM * p:LM * p + LM], ql_bd[:, half, q:q + 2, :].rearrange("p h j -> p (h j)"),
                                    klt[:, half, :], start=True, stop=True)
                ins.then_inc(S["s2_ps"], 1)
                for bank, part, t, half in ((6, 2, ql_bd, 0), (7, 3, ql_bd, 1), (2, 0, kl_bd, 0), (5, 1, kl_bd, 1)):
                    pe.matmul(ps[:, bank, :], mt[:, part, :], t[:, half, :, :].rearrange("p h j -> p (h j)"),
                              start=True, stop=True).then_inc(S["g_ps"], 1)
                pe.wait_ge(S["xbd_ready"], b + 1)
                pe.wait_ge(S["coef_act"], 5 * b + 5)
                pe.wait_ge(S["coef_dve"], 4 * b + 4)
                for i in range(2):
                    for j in range(4):
                        ins = pe.transpose(ps[:, i, 128 * j:128 * j + 128], xbd[:, 4 * i + j, :], ident)
                    ins.then_inc(S["xt_ps"], 1)

            def pseudo_inverse(b):
                act_n, dve_n, units = [0, 0], [0, 0], [0]
                pe.wait_ge(S["xt_sb"], 2 * b + 2)
                for s, k, half, fill in pinv_steps():
                    def product(i, lhs, rhs, done=False):
                        for j in range(4):
                            n = 4 * half + j
                            ins = pe.matmul(ps[:, 3 * half + i, 128 * j:128 * j + 128], lhs[:, n, :], rhs[:, n, :],
                                            start=True, stop=True)
                        if done:
                            ins.then_inc(S[f"pi_pe{half}"], 1)

                    pe.wait_ge(S[f"pi_act{half}"], past(PI_ACT * b + act_n[half]))
                    pe.wait_ge(S[f"pi_dve{half}"], past(PI_DVE * b + dve_n[half]))
                    if s == "init":
                        product(0, xt, xbd)
                        product(1, xbd, xt, True)
                        act_n[half] += 2
                        dve_n[half] += 1
                    elif s == "square":
                        product(0, ym, yt, True)
                        act_n[half] += 1
                    elif s == "poly":
                        product(1, y2t, y7, True)
                        dve_n[half] += 1
                    elif k < ITERS - 1:
                        if k == 0:
                            pe.wait_ge(S["g_ready"], 4 * b + 3 + half)
                        product(0, yt, qm)
                        product(1, qm, yt)
                        product(2, qm, vt if k else xt, True)
                        act_n[half] += 3
                        dve_n[half] += 1
                    else:
                        product(2, qm, vt, True)
                        act_n[half] += 1
                    for p, d in fill:
                        if units[0] == 0:
                            pe.wait_ge(S["g_ready"], 4 * b + 2)
                        if units[0] or not first(b):
                            pe.wait_ge(S["s3m_used"], past(len(score_units()) * b + units[0]))
                        units[0] += 1
                        for i in range(2):
                            if p is None:
                                for j in range(4):
                                    ins = pe.matmul(ps[:, 6 + i, 128 * j:128 * j + 128],
                                                    ql_bd[:, i, 2 * j:2 * j + 2, :].rearrange("p h j -> p (h j)"),
                                                    qk_xt[:, 2 + i, :], start=True, stop=True)
                            else:
                                ins = pe.matmul(ps[:, 6 + i, :], g3[:, 128 * p:128 * p + 128],
                                                coef_t[:, 1024 * d + 512 * i:1024 * d + 512 * i + 512],
                                                start=True, stop=True)
                        ins.then_inc(S["s3m_pe"], 1)
                pe.wait_ge(S["m3_ready"], b + 1)
                for p in range(PAIRS):
                    ins = pe.matmul(ps[32:64, 6 + p // 4, 128 * (p % 4):128 * (p % 4) + 128], m3z[:, p, :], ident,
                                    start=True, stop=True)
                ins.then_inc(S["m3_ps"], 1)
                pe.wait_ge(S["g3_shift"], b + 1)
                for half in range(2):
                    pe.wait_ge(S[f"pi_act{half}"], past(PI_ACT * (b + 1)))

            def landmark_values(b):
                def score(n, j, text=False):
                    for i in range(2):
                        o = ps[:, 2 * (j % 2) + i, :]
                        ins = pe.matmul(o, coef_t[:, ds(128 * n, 128)], g3[:, 512 * i:512 * i + 512],
                                        start=True, stop=not text)
                        if text:
                            ins = pe.matmul(o, qk_xt[:, 2 + i, :], ql_bd[:, i, :, :].rearrange("p h j -> p (h j)"),
                                            start=False, stop=True)
                    ins.then_inc(S["s3_pe"], 1)

                def gather(j, slot, start, stop):
                    for i in range(2):
                        q = 2 * (j % 2) + i
                        ins = pe.matmul(ps[32 * q:32 * q + 32, 4, :], cfw[:, slot, :], p3[:, j, 512 * i:512 * i + 512],
                                        start=start, stop=stop, skip_group_check=True)
                    return ins

                def two(b, k, half, start, pair):
                    pe.wait_ge(S["cfw_ready"], CH * b + k + 1)
                    pe.wait_ge(S["s3_exp"], TILES * b + 4 * k + 2 * pair + 2)
                    stop = isinstance(k, int) and k == CH - 1 and pair == 1
                    gather(2 * pair, 4 * half + 2 * pair, start, False)
                    gather(2 * pair + 1, 4 * half + 2 * pair + 1, start, stop).then_inc(S["pv3_pe"], 1)

                def chunk(k, half):
                    for j in range(4):
                        n = 4 * k + j
                        if not (isinstance(k, int) and k == 0 and j < 2):
                            pe.wait_ge(S["s3_exp"], TILES * b + n - 1)
                        score(n, j)
                        if j == 1 and not first(k):
                            two(b, k - 1, 1 - half, False, 1)
                        if j == 3:
                            two(b, k, half, first(k), 0)

                chunk(0, 0)
                chunk(1, 1)
                with pe.Fori(1, CH // 2) as i:
                    k = 2 * i
                    chunk(k, 0)
                    chunk(k + 1, 1)
                pe.wait_ge(S["s3_exp"], TILES * b + NT - 1)
                score(NT, 0, True)
                two(b, CH - 1, 1, False, 1)
                pe.wait_ge(S["s3_exp"], TILES * (b + 1))
                for i in range(2):
                    ins = pe.matmul(ps[32 * i:32 * i + 32, 4, :], cf[:, NT, :], p3[:, 0, 512 * i:512 * i + 512],
                                    start=False, stop=True, skip_group_check=True)
                ins.then_inc(S["pv3_pe"], 1)
                pe.wait_ge(S["c3_sb"], b + 1)
                for p in range(PAIRS):
                    o = ps[:, 5, 34 * p:34 * p + 34]
                    pe.matmul(o, c3[:, 128 * (p % 4):128 * (p % 4) + 128], v4x[:, p, :], start=True, stop=True)
                    ins = pe.matmul(o[:, 0:32], p3[:, 0, 128 * p:128 * p + 128], qkv_x[:, 512 + 32 * p:544 + 32 * p],
                                    start=False, stop=True, skip_group_check=True)
                ins.then_inc(S["o3_ps"], 1)
                pe.wait_ge(S["w3_ready"], b + 1)
                for p in range(PAIRS):
                    ins = pe.matmul(ps[:, 6, 16 * p:16 * p + 16], vt[:, p, :], w3[:, p, :], start=True, stop=True)
                ins.then_inc(S["z_ps"], 1)
                pe.wait_ge(S["z_ready"], b + 1)

            def row_scores(b, k, j):
                t = 4 * (C9 * b + k) + j
                if not first(t):
                    pe.wait_ge(S["s1m_used"], past(t))
                for i in range(2):
                    ins = pe.matmul(ps[:, i, :], coef_t[:, ds(512 * k + 128 * j, 128)], g1[:, 512 * i:512 * i + 512],
                                    start=True, stop=True)
                ins.then_inc(S["s1m_pe"], 1)

            def text_row_scores(b):
                pe.wait_ge(S["s1m_used"], past(4 * (C9 * b + CH)))
                for i in range(2):
                    ins = pe.matmul(ps[:, i, :], qk_xt[:, i, :], kl_bd[:, i, :, :].rearrange("p h j -> p (h j)"),
                                    start=True, stop=True)
                ins.then_inc(S["s1m_pe"], 4)

            def max_rows(b, k, n):
                c = C9 * b + k
                pe.wait_ge(S["s1m_used"], past(4 * c + 4))
                for j in range(n):
                    ins = pe.transpose(psb(0)[MAXROW:MAXROW + H, 128 * j:128 * j + 128], m1[:, j, :], identb[:, :])
                ins.then_inc(S["m1t_ps"], 1)

            def scores(b, k, g, pps, w, text):
                c = C9 * b + k
                for pp in pps:
                    e = 8 * c + 4 * g + pp
                    p = 4 * g + pp
                    if not (isinstance(k, int) and k == 0 and g == 0 and pp < 2):
                        pe.wait_ge(S["p1_ready"], e - 1)
                    o = ps[:, 2 + pp % 2, 0:w]
                    ins = pe.matmul(o, g1[:, 128 * p:128 * p + 128], coef_t[:, ds(512 * k, w)], start=True, stop=not text)
                    if text:
                        ins = pe.matmul(o, kl_bd[:, g, 2 * pp:2 * pp + 2, :].rearrange("p h j -> p (h j)"),
                                        qk_xt[:, g, :], start=False, stop=True)
                    ins.then_inc(S["s1_pe"], 1)

            def values(b, k, g, w):
                c = C9 * b + k
                pe.wait_ge(S["p1_ready"], 8 * c + 4 * g + 4)
                pe.wait_ge(S["u_ready"], past(2 * c + g))
                if g == 0:
                    pe.wait_ge(S["d_ready"], past(c))
                for q in range(4):
                    pe.matmul(ps[32 * q:32 * q + 32, 4, 0:w], z_bd[:, 4 * g + q, :], p1[:, g, q, 0:w],
                              start=True, stop=True)
                for q in range(4):
                    a = LAYOUT["onehot"][0] + 32 * (4 * g + q)
                    ins = pe.matmul(ps[32 * q:32 * q + 32, 5, 0:w], sb_const[:, a:a + 32], p1[:, g, q, 0:w],
                                    start=g == 0, stop=g == 1, skip_group_check=True)
                ins.then_inc(S["ud_pe"], 1)

            def turn_denominators(b, kp, n):
                cp = C9 * b + kp
                pe.wait_ge(S["d_ready"], past(cp + 1))
                for j in range(n):
                    ins = pe.transpose(ps[:, 7, 128 * j:128 * j + 128], d_sb[:, 128 * j:128 * j + 128], ident)
                ins.then_inc(S["dt_ps"], 1)

            def turn_reciprocals(b, kp, g, n):
                cp = C9 * b + kp
                pe.wait_ge(S["rdb_ready"], past(cp + 1))
                pe.wait_ge(S["o_ready"], 2 * cp + g) if g else pe.wait_ge(S["dt_used"], cp + 1)
                for j in range(n):
                    ins = pe.transpose(ps[:, 7, 128 * j:128 * j + 128],
                                       rd_all[:, j, 8 * g:8 * g + 8, :].rearrange("p h d -> p (h d)"), ident)
                ins.then_inc(S["rdt_ps"], 1)

            def project(b, kp, i, tiles, text=False):
                cp = C9 * b + kp
                if tiles[0] == 0:
                    pe.wait_ge(S["o_ready"], 2 * cp + 2)
                    pe.wait_ge(S["out_ready"], past(2 * cp + i))
                for jj in tiles:
                    j = 2 * i + jj
                    o = ps[:, 6, 256 * jj:256 * jj + 256]
                    if not text:
                        pe.matmul(o, coef_t[:, ds(512 * kp + 128 * j, 128)], res_w[:, :], start=True, stop=False)
                    for g in range(2):
                        ins = pe.matmul(o, o_sb[:, g, 128 * j:128 * j + 128], wo[:, g, :], start=text and g == 0,
                                        stop=g == 1)
                if text or tiles[-1] == 1:
                    ins.then_inc(S["out_ps"], 2 if text else 1)

            def chunk(b, k, w, prev, before, nxt):
                text = isinstance(k, int) and k == CH
                text_next = nxt and isinstance(k, int) and k == CH - 1
                rows = nxt and not text_next
                if prev:
                    turn_denominators(b, k - 1, 4)
                pe.wait_ge(S["m1t_sb"], C9 * b + k + 1)
                scores(b, k, 0, (0, 1), w, text)
                if text_next:
                    text_row_scores(b)
                elif rows:
                    row_scores(b, k + 1, 0)
                if before:
                    project(b, k - 2, 1, (0, 1))
                scores(b, k, 0, (2, 3), w, text)
                if prev:
                    turn_reciprocals(b, k - 1, 0, 4)
                scores(b, k, 1, (0,), w, text)
                if rows:
                    row_scores(b, k + 1, 1)
                values(b, k, 0, w)
                scores(b, k, 1, (1,), w, text)
                if prev:
                    turn_reciprocals(b, k - 1, 1, 4)
                scores(b, k, 1, (2,), w, text)
                if rows:
                    row_scores(b, k + 1, 2)
                scores(b, k, 1, (3,), w, text)
                if prev:
                    project(b, k - 1, 0, (0,))
                if rows:
                    row_scores(b, k + 1, 3)
                values(b, k, 1, w)
                if nxt:
                    max_rows(b, k + 1, 1 if text_next else 4)
                if prev:
                    project(b, k - 1, 0, (1,))

            def batch(b):
                pe.wait_ge(S["out_ready"], past(2 * C9 * b))
                setup_sequence(b)
                pseudo_inverse(b)
                landmark_values(b)
                for j in range(4):
                    row_scores(b, 0, j)
                max_rows(b, 0, 4)
                chunk(b, 0, 512, False, False, True)
                chunk(b, 1, 512, True, False, True)
                with pe.Fori(1, CH // 2 - 1) as i:
                    chunk(b, 2 * i, 512, True, True, True)
                    chunk(b, 2 * i + 1, 512, True, True, True)
                chunk(b, CH - 2, 512, True, True, True)
                chunk(b, CH - 1, 512, True, True, True)
                chunk(b, CH, P, True, True, False)
                project(b, CH - 1, 1, (0, 1))
                turn_denominators(b, CH, 1)
                turn_reciprocals(b, CH, 0, 1)
                turn_reciprocals(b, CH, 1, 1)
                project(b, CH, 0, (0,), True)

            with pe.Fori(0, NB) as b:
                batch(b)

            pe.wait_ge(S["out_ready"], past(2 * C9 * NB))
            pe.wait_ge(S["f_we"], 1)
            for i in range(4):
                for j in range(4):
                    ins = pe.transpose(ps[0:E, i, 128 * j:128 * j + 128], eq[:, 0, 4 * i + j, :], ident)
                ins.then_inc(S["f_wet_ps"], 1)

            def turn_rows(c):
                pe.wait_ge(S["f_xn"], c + 1)
                for i in range(2):
                    for k in range(2):
                        for j in range(2):
                            ins = pe.transpose(ps[:, 6 + i, 256 * k + 128 * j:256 * k + 128 * j + 128],
                                               xn[:, 2 * i + j, 128 * k:128 * k + 128], ident)
                    ins.then_inc(S["f_xnt_ps"], 1)

            def out_rows(c):
                pe.wait_ge(S["f_y2"], 4 * c + 4)
                for i in range(2):
                    for jj in range(2):
                        for p in range(E // 2):
                            a = 128 * (2 * i + jj)
                            ins = pe.matmul(ps[:, 6 + i, 256 * jj:256 * jj + 256], y2[:, p, a:a + 128], w2b_s[:, p, :],
                                            start=p == 0, stop=p == 3)
                    ins.then_inc(S["f_out_ps"], 1)

            def experts(c, last):
                pe.wait_ge(S["f_xnt"], 2 * c + 2)
                for p in range(E // 2):
                    if p >= 2:
                        pe.wait_ge(S["f_mid"], 4 * c + p - 1)
                    elif not first(c):
                        pe.wait_ge(S["f_y2"], 4 * c - 1 + p)
                    for k in range(2):
                        ins = pe.matmul(ps[:, 4 + p % 2, :], w1a_s[:, k, 128 * p:128 * p + 128], xn_t[:, k, :],
                                        start=k == 0, stop=k == 1)
                    ins.then_inc(S["f_l0"], 1)
                if not first(c):
                    out_rows(c - 1)
                for p in range(E // 2):
                    if not (first(c) and p == 0):
                        pe.wait_ge(S["f_wx"], 4 * c + p)
                    if p == 0 and not first(c):
                        pe.wait_ge(S["f_out"], 2 * c)
                    if p == 3 and not last:
                        pe.wait_ge(S["f_xnt"], 2 * c + 3)
                    pe.matmul(ps[:, 6, :], con("selE")[:, 128 * p:128 * p + 128], we_t[:, ds(512 * c, 512)],
                              start=True, stop=True).then_inc(S["f_wx_ps"], 1)
                    if p == 2 and not last:
                        pe.wait_ge(S["f_wx"], 4 * c + p + 1)
                        turn_rows(c + 1)
                    pe.wait_ge(S["f_mid"], 4 * c + p + 1 if p < 2 else 4 * c + 4)
                    if p < 2:
                        pe.wait_ge(S["f_mid"], 4 * c + p + 3)
                    else:
                        pe.wait_ge(S["f_y2"], 4 * c + p - 1)

                    def second(f):
                        u = (4 * c + p) * FB + f
                        pe.wait_ge(S["f_gelu"], 2 * u + 2)
                        for e in range(2):
                            a = 64 * (2 * p + e)
                            ins = pe.matmul(ps[64 * e:64 * e + 64, 4 + p % 2, :], w2a_s[:, f, a:a + 64],
                                            hid[:, e, f % 2, :], start=f == 0, stop=f == FB - 1)
                        ins.then_inc(S["f_l2"], 1)

                    for f in range(FB):
                        u = (4 * c + p) * FB + f
                        if not (first(c) and p == 0 and f < 2):
                            pe.wait_ge(S["f_gelu"], 2 * u - 2)
                        for e in range(2):
                            pe.matmul(ps[:, 2 * (f % 2) + e, :], w1b_z[:, 2 * p + e, 128 * f:128 * f + 128],
                                      mid[:, p, :], start=True, stop=True).then_inc(S["f_l1"], 1)
                        if f:
                            second(f - 1)
                    second(FB - 1)
            pe.wait_ge(S["f_in"], 16 * 5)
            pe.wait_ge(S["f_zero"], 2)
            turn_rows(0)
            pe.wait_ge(S["f_wet"], 4)
            experts(0, False)
            with pe.Fori(1, FT // 4 - 1) as c:
                experts(c, False)
            experts(FT // 4 - 1, True)
            out_rows(FT // 4 - 1)


def kernel(x, txt, L0_tok_kernel, L0_tok_bias, L0_attn_Wqkv, L0_attn_bqkv, L0_attn_Wout, L0_attn_bout,
           L0_ffn_expert_weights, L0_ffn_expert_indices, L0_ffn_w1_A, L0_ffn_w1_B, L0_ffn_w2_A, L0_ffn_w2_B):
    import concourse.bacc as bacc
    from concourse.bass_utils import run_bass_kernel_spmd

    consts, member = constants()
    arrays = {
        "x": np.asarray(x).reshape(NB, 2, P, 48), "txt": np.asarray(txt),
        "tok_kernel": np.asarray(L0_tok_kernel), "tok_bias": np.asarray(L0_tok_bias).reshape(1, D),
        "wqkv": np.asarray(L0_attn_Wqkv), "bqkv": np.asarray(L0_attn_bqkv).reshape(1, 3 * D),
        "wout": np.asarray(L0_attn_Wout), "bout": np.asarray(L0_attn_bout).reshape(1, D),
        "ew": np.asarray(L0_ffn_expert_weights).reshape(P, 2 * FT),
        "ei": np.asarray(L0_ffn_expert_indices).reshape(P, 2 * FT),
        "w1a_t": np.asarray(L0_ffn_w1_A).T, "w1b": np.asarray(L0_ffn_w1_B),
        "w2a_t": np.asarray(L0_ffn_w2_A).T, "w2b": np.asarray(L0_ffn_w2_B),
        "consts": consts, "member": member,
    }
    arrays = {k: np.ascontiguousarray(v) for k, v in arrays.items()}
    nc = bacc.Bacc("TRN2", target_bir_lowering=False, num_devices=1)
    args = [nc.dram_tensor(k, v.shape, mybir.dt.from_np(v.dtype), kind="ExternalInput").ap() for k, v in arrays.items()]
    out = nc.dram_tensor("out", (NB, NG + NX, D), F32, kind="ExternalOutput").ap()
    build(nc, *args, out)
    r = run_bass_kernel_spmd(nc, [arrays], core_ids=[0])
    return r.results[0]["out"]
```

```python
import math
from contextlib import ExitStack

import numpy as np
import concourse.bass as bass
from concourse import mybir

F32 = mybir.dt.float32
BF16 = mybir.dt.bfloat16
ALU = mybir.AluOpType
ACT = mybir.ActivationFunctionType
AX = mybir.AxisListType
ds = bass.ds

P = 128
NB = 4
NG = 4096
NX = 128
NT = NG // P
TILES = NT + 1
CH = NG // 512
D = 256
H = 16
DH = D // H
LM = 64
GROUP = (NG + NX) // LM
STEPS = 16
PAIRS = H // 2
ITERS = 6
EPS = 1e-5
FFN_T = 2048
FT = FFN_T // P
E = 8
RANK = 64
FF = 1024
FB = FF // P

A_COLS = {1: (0, 64, 96), 2: (4, 68), 3: (8,)}
B_COLS = {1: (12, 72, 100), 2: (14, 74), 3: (16,)}
MAXROW = 32
ONEROW = 48
WEIGHT_ROWS = (0, 32, 64)

LAYOUT = {}
_at = 0
for _name, _n in (("ident", 128), ("trig", 32), ("mask8", 8), ("sel3", 128), ("sel1", 128), ("e3", 4),
                  ("selV", 256), ("col32", 2), ("onehot", 256), ("negind", 1024), ("selE", 512), ("iota8", 8)):
    LAYOUT[_name] = (_at, _at + _n)
    _at += _n
NCONST = _at


def constants():
    c = np.zeros((P, NCONST), np.float32)

    def part(name):
        a, b = LAYOUT[name]
        return c[:, a:b]

    part("ident")[:] = np.eye(P, dtype=np.float32)
    theta = np.linspace(0.0, 2.0 * np.pi, STEPS, dtype=np.float32).astype(np.float64)
    part("trig")[:, 0:16] = np.cos(theta)
    part("trig")[:, 16:32] = np.sin(theta)
    for ch in range(P):
        part("mask8")[ch, ch // DH] = 1.0
    for n in (1, 2, 3):
        for col in B_COLS[n]:
            part("sel3")[0, col] = 1.0
            part("sel3")[1, col + 1] = 1.0
    for col in A_COLS[1]:
        part("sel3")[2, col + 3] = 1.0
        part("sel1")[0, col + 3] = 1.0
    part("e3")[0, 3] = 1.0
    sel_v = part("selV").reshape(P, 2, 128)
    for half in range(2):
        for k in range(4):
            for q in (half, half + 2):
                sel_v[k, half, 32 * q + k] = 1.0
        for q in (half, half + 2):
            part("col32")[32 * q + 3, half] = 1.0
    one = part("onehot").reshape(P, PAIRS, 32)
    for p in range(PAIRS):
        one[0:64, p, 2 * p] = 1.0
        one[64:128, p, 2 * p + 1] = 1.0
    neg = part("negind").reshape(P, H, LM)
    for h in range(H):
        neg[MAXROW + h, h, :] = -1.0
    sel_e = part("selE").reshape(P, 4, 128)
    for e in range(E):
        for first_row in WEIGHT_ROWS:
            sel_e[first_row + e, e // 2, 64 * (e % 2):64 * (e % 2) + 64] = 1.0
    part("iota8")[:] = np.arange(E, dtype=np.float32)
    member = np.zeros((P, TILES, LM), np.float32)
    for n in range(TILES):
        for p in range(P):
            token = NG + p if n == NT else (n // 16) * 2048 + p * 16 + n % 16
            member[p, n, token // GROUP] = 1.0 / GROUP
    return c, member.reshape(P, TILES * LM)


def build(nc, x, txt, tok_kernel, tok_bias, wqkv, bqkv, wout, bout, ew, ei, w1a_t, w1b, w2a_t, w2b,
          consts, member, out):
    ctx = ExitStack()
    with ctx:
        def sb(name, shape, dt=F32):
            return ctx.enter_context(nc.sbuf_tensor(name, shape, dt))

        def sem(name):
            return ctx.enter_context(nc.semaphore(name))

        ps = ctx.enter_context(nc.psum_tensor("ps", [P, 8, 512], F32))

        def psb(i):
            return ps[:, i, :].bitcast(BF16)

        arena = sb("arena", [P, 18432])
        taken = [0]

        def view(shape, dt=F32):
            n = int(np.prod(shape[1:]))
            words = n if dt == F32 else n // 2
            v = arena[:, taken[0]:taken[0] + words]
            taken[0] += words
            if dt != F32:
                v = v.bitcast(dt)
            if len(shape) == 3:
                v = v.rearrange("p (a b) -> p a b", b=shape[2])
            if len(shape) == 4:
                v = v.rearrange("p (a b c) -> p a b c", b=shape[2], c=shape[3])
            return v

        sb_const = sb("sb_const", [P, NCONST])
        sb_member = sb("sb_member", [P, TILES, LM])

        def con(name):
            a, b = LAYOUT[name]
            return sb_const[:, a:b]

        ident = con("ident")
        identb = sb("identb", [P, P], BF16)
        eps_col = sb("eps_col", [P, 1])
        halfpi = sb("halfpi", [P, 1])
        waiter = sb("waiter", [P, 1])
        ones_row = sb("ones_row", [1, P])
        mean_w = sb("mean_w", [P, P])
        wq = sb("wq", [P, 2, 3 * D])
        bq = sb("bq", [1, 3 * D])
        wo = sb("wo", [P, 2, D])
        kb = sb("kb", [3, D])
        kbc = sb("kbc", [3, D])
        ksum = sb("ksum", [3, 2])
        bo = sb("bo", [1, D])
        bout_all = sb("bout_all", [P, D])
        bq_all = sb("bq_all", [P, 2 * D])
        kt4 = sb("kt4", [P, 2, 4])
        prod = sb("prod", [P, 2, 6])
        gram = sb("gram", [P, 6])
        m4 = sb("m4", [4, 3 * D])
        mt = sb("mt", [P, 4, P])
        v4x = sb("v4x", [P, PAIRS, 34])
        split_r = sb("split_r", [P, 512])
        res_w = sb("res_w", [P, D], BF16)
        xb = sb("xb", [P, NT, 3])
        ang = [view([P, NT, STEPS]) for _ in range(2)]
        rnd = [view([P, NT, STEPS]) for _ in range(2)]
        sin_a = view([P, NT, STEPS])
        abs_a = view([P, NT, STEPS])
        re = view([P, NT, STEPS])
        im = view([P, NT, STEPS])
        tre = view([P, 4, NT, 8])
        st = sb("st", [P, 4, NT])
        reim = sb("reim", [P, NT, 2])
        sd = sb("sd", [P, NT])
        rstd = sb("rstd", [P, NT])
        cf = sb("cf", [P, TILES, 32])
        ce = sb("ce", [P, NT, 4])
        tc = view([P, TILES, P], BF16)
        coef_t = sb("coef_t", [P, TILES * P], BF16)
        tx = sb("tx", [P, D])
        txr = sb("txr", [P, D])
        txn = sb("txn", [P, D])
        txstat = sb("txstat", [P, 6])
        txmv = sb("txmv", [P, 2])
        txsd = sb("txsd", [P, 2])
        txn_t = sb("txn_t", [P, 2, P])
        qkv_x = sb("qkv_x", [P, 3 * D])
        qk_xt = sb("qk_xt", [P, 4, P])
        lm_c = sb("lm_c", [4, LM])
        klt = sb("klt", [P, 2, LM])
        kl_bd = sb("kl_bd", [P, 2, 8, LM])
        ql_bd = sb("ql_bd", [P, 2, 8, LM])
        g1 = sb("g1", [P, H * LM], BF16)
        g3 = sb("g3", [P, H * LM], BF16)
        s2 = sb("s2", [P, PAIRS, LM])
        s2m = sb("s2m", [P, 2, PAIRS])
        bd = [P, PAIRS, P]
        xbd, xt, ym, yt, y2t, qm, vt, ylin, y7 = (
            view(bd) for _ in range(9))
        id7 = sb("id7", [P, P])
        id13 = sb("id13", [P, P])
        m3part = sb("m3part", [P, PAIRS, CH + 1])
        m3z = sb("m3z", [P, PAIRS, 32])
        c3 = sb("c3", [P, 512])
        w3 = sb("w3", [P, PAIRS, DH])
        w3r = sb("w3r", [P, PAIRS])
        z_bd = sb("z_bd", [P, PAIRS, 32])
        prob = sb("prob", [P, 2, 4, 512])
        p3 = prob[:, :, :, :].rearrange("p a b c -> p (a b c)").rearrange("p (n c) -> p n c", n=4)
        p1 = prob
        m1 = sb("m1", [P, 4, H], BF16)
        u_sb = sb("u_sb", [P, 2, 2, 512])
        d_sb = sb("d_sb", [P, 512])
        d_t = sb("d_t", [P, 4, H])
        rd = sb("rd", [P, 4, H])
        rd_all = sb("rd_all", [P, 4, H, DH])
        o_sb = sb("o_sb", [P, 2, 512])
        out_sb = sb("out_sb", [P, 2, 4, D])

        taken[0] = 0
        w1b_z = view([P, E, FF])
        w2a_s = view([P, FB, E * RANK])
        w2b_s = view([P, E // 2, D])
        w1a_s = view([P, 2, E * RANK])
        x1 = view([P, FT, D])
        assert taken[0] == 18432
        spare = prob[:, :, :, :].rearrange("p a b c -> p (a b) c")
        hid = spare[:, 0:4, :].rearrange("p (e r) c -> p e r c", e=2)
        y2 = spare[:, 4:8, :]
        mid = u_sb[:, :, :, :].rearrange("p a b c -> p (a b) c")
        xn = kl_bd[:, :, :, :].rearrange("p a h j -> p (a h j)").rearrange("p (n c) -> p n c", n=4)
        xn_t = rd_all[:, :, :, :].rearrange("p n h d -> p (n h d)").rearrange("p (k c) -> p k c", k=2)
        wx = split_r
        wt = ql_bd[:, :, :, :].rearrange("p a h j -> p (a h j)").bitcast(BF16).rearrange("p (n c) -> p n c", n=FT)
        we_t = coef_t[:, 0:FFN_T]
        sel_e = mt[:, :, :].rearrange("p n c -> p (n c)").bitcast(BF16)[:, 0:4 * P]
        ew_s = sb("ew_s", [P, FT, 2])
        ei_s = sb("ei_s", [P, FT, 2], mybir.dt.int32)
        ei_f = sb("ei_f", [P, FT, 2])
        eq = txn[:, :].rearrange("p (k n e) -> p k n e", k=2, n=FT)
        fst = sb("fst", [P, FT, 6])
        fmv = sb("fmv", [P, FT, 2])
        fsd = sb("fsd", [P, 2, FT])

        s_const = sem("s_const")
        s_w = sem("s_w")
        s_zero = sem("s_zero")
        s_xin = sem("s_xin")
        s_txin = sem("s_txin")
        pool_step = sem("pool_step")
        dve_step = sem("dve_step")
        S = {n: sem(n) for n in """
            kbc_ready kt_ps kt4_ready gram_ps m4_ps m4_sb mt_ps v4_ps bout_ps setup_sb gram_sb
            ang0_ready ang1_ready sin_ready var_ready sd_ready txvar_ready tc_ready tx_used
            txn_ready txnt_ps txnt_sb coef_ps coef_act coef_dve qkx_ps qkx_sb qkx_bias lm_ps lm_sb qkxt_ps qkxt_sb
            qkl_ps klbd_ready qlbd_ready g_ps g_first g_ready s2_ps s2_sub s2_exp xbd_ready xt_ps xt_sb
            pi_pe0 pi_pe1 pi_act0 pi_act1 pi_dve0 pi_dve1 s3m_pe s3m_used m3_ready m3_ps g3_shift
            s3_pe0 s3_pe1 s3_exp0 s3_exp1 pv3_pe c3_sb o3_ps w3_ready z_ps z_ready
            s1m_pe s1m_used m1t_ps m1t_sb s1_pe p1_ready ud_pe u_ready d_ready dt_ps dt_used rd_ready rdb_ready
            rdt_ps o_ready out_ps out_ready out_stored0 out_stored1
            f_zero f_in f_x f_e f_we f_wet_ps f_wet f_var f_sd f_xn f_xnt_ps f_xnt f_l0 f_mid f_wx_ps f_wx f_l1 f_gelu
            f_l2 f_y2 f_out_ps f_out f_stored""".split()}
        C9 = CH + 1
        PI_PE = 1 + 3 * ITERS
        PI_ACT = 2 + ITERS + 3 * (ITERS - 1) + 1
        PI_DVE = ITERS + ITERS

        G_ORDER = ((g3, 6, 0), (g3, 7, 1), (g1, 2, 0), (g1, 5, 1))

        COEF_BANKS = (0, 1, 6, 7)

        def first(v):
            return isinstance(v, int) and v == 0

        FROM_ONE = """rdt_ps ud_pe rdb_ready out_ps dt_ps out_stored0 out_stored1 f_stored pi_act0 pi_act1
            pi_dve0 pi_dve1 s1m_used u_ready d_ready out_ready""".split()
        started = sb("started", [P, len(FROM_ONE)])

        def past(n):
            return n + 1

        UNITS = [(p, k) for p in range(PAIRS) for k in range(CH)] + [(None, 0), (None, 1)]

        UNIT_RATE, TILE_RATE = ((2, 2, 2), 1), ((2, 2, 2), 2)
        ROW_GAP = 1

        def pinv_steps():
            steps = [("init", 0)] + [(s, k) for k in range(ITERS) for s in ("square", "poly", "next")]
            units = [("unit", u) for u in range(len(UNITS))]
            rest = [[("max", None)], [("shift", None)]]
            tiles = [("tile", n) for n in range(TILES)]
            plan = []
            for s, k in steps:
                for half in range(2):
                    within = []
                    if not units and rest:
                        after = rest.pop(0)
                    else:
                        queue, rate = (units, UNIT_RATE) if units else (tiles, TILE_RATE)
                        fills = []
                        for m in rate[0] if s == "next" and k < ITERS - 1 else (rate[1],):
                            fills.append(queue[:m])
                            del queue[:m]
                        *within, after = fills
                    plan.append((s, k, half, within, after))
            rows = [("row", j) for j in range(4)]
            while tiles or rows:
                plan[-1][4].extend(tiles[:ROW_GAP] + rows[:1])
                del tiles[:ROW_GAP], rows[:1]
            assert not units and not rest
            return plan

        def pinv_bank(half, i):
            return ps[:, (3 * half + i, 2)[i == 2], :].rearrange("p (n c) -> p n c", n=4)

        def angles(engine, step, i, scratch):
            trig = con("trig")[:, 16 * i:16 * i + 16].rearrange("p (o k) -> p o k", o=1).to_broadcast([P, NT, STEPS])
            period = (4 * math.pi, math.pi)[i]
            magic = 1.5 * 2.0 ** 23
            a, turns, multiple = ang[i][:, :, :], scratch[0][:, :, :], scratch[1][:, :, :]
            c1 = math.floor(period * 32) / 32

            def col(j):
                return xb[:, :, j:j + 1].to_broadcast([P, NT, STEPS])

            step(engine.tensor_tensor(a, col(2), trig, ALU.mult))
            step(engine.tensor_tensor(a, a, col(i), ALU.add), True)
            step(engine.tensor_scalar(turns, a, 1.0 / period, magic, ALU.mult, ALU.add), True)
            step(engine.tensor_scalar(multiple, turns, -magic, -c1, ALU.add, ALU.mult))
            step(engine.tensor_tensor(a, a, multiple, ALU.add), True)
            step(engine.tensor_scalar(multiple, turns, -magic, c1 - period, ALU.add, ALU.mult))
            step(engine.tensor_tensor(a, a, multiple, ALU.add), True)
            lim = float(np.nextafter(np.float32(period / 2), np.float32(0)))
            engine.tensor_scalar(a, a, lim, -lim, ALU.min, ALU.max).then_inc(S[f"ang{i}_ready"], 1)

        def products(engine, step, b, waiting):
            engine.wait_ge(S["sin_ready"], 4 * b + 4)
            step(engine.tensor_tensor(im[:, :, :], sin_a[:, :, :], im[:, :, :], ALU.mult))
            w = STEPS // 2
            while w:
                last = w == 1
                r0, r1, i0, i1 = re[:, :, 0:w], re[:, :, w:2 * w], im[:, :, 0:w], im[:, :, w:2 * w]
                t = [tre[:, j, :, 0:w] for j in range(4)]
                for o, (p_, q_) in zip(t, ((r0, r1), (i0, i1), (r0, i1), (i0, r1))):
                    step(engine.tensor_tensor(o, p_, q_, ALU.mult))
                if last:
                    if not first(b):
                        engine.wait_ge(S["tc_ready"], b)
                    r0, i0 = reim[:, :, 0:1], reim[:, :, 1:2]
                step(engine.tensor_tensor(r0, t[0], t[1], ALU.subtract))
                step(engine.tensor_tensor(i0, t[2], t[3], ALU.add), last)
                w //= 2
            r, i = reim[:, :, 0], reim[:, :, 1]
            u, v, w_, x_ = (st[:, j, :] for j in range(4))
            step(engine.tensor_scalar(u, r, gram[:, 0:1], gram[:, 5:6], ALU.mult, ALU.add), True)
            step(engine.tensor_scalar(w_, i, gram[:, 3:4], 0.0, ALU.mult, ALU.add))
            step(engine.tensor_tensor(u, u, w_, ALU.add))
            step(engine.tensor_tensor(u, u, r, ALU.mult), True)
            step(engine.tensor_scalar(v, i, gram[:, 1:2], gram[:, 4:5], ALU.mult, ALU.add))
            step(engine.tensor_tensor(v, v, i, ALU.mult))
            step(engine.tensor_tensor(u, u, v, ALU.add))
            if not first(b):
                engine.wait_ge(S["sd_ready"], 2 * b)
            waiting()
            engine.tensor_scalar(x_, u, gram[:, 2:3], 0.0, ALU.add, ALU.max).then_inc(S["var_ready"], 1)

        block = ctx.enter_context(nc.Block())

        @block.sync
        def _(sp):
            sp.dma_start(sb_const[:, :], consts).then_inc(s_const, 16)

            def load_points(b):
                if not first(b):
                    for i in range(2):
                        sp.wait_ge(S[f"ang{i}_ready"], b)
                for half in range(2):
                    sp.dma_start(xb[:, 16 * half:16 * half + 16, :],
                                 x[ds(b, 1), half, :, :].rearrange("o p (n c) -> p (o n) c", c=3)).then_inc(s_xin, 16)

            def load_text(b):
                if not first(b):
                    sp.wait_ge(S["tx_used"], b)
                sp.dma_start(tx[:, :], txt[ds(b, 1), :, :].rearrange("o p n -> p (o n)")).then_inc(s_txin, 16)

            load_points(0)
            sp.dma_start(wq[:, :, :], wqkv.rearrange("(k p) n -> p k n", p=P)).then_inc(s_w, 16)
            sp.dma_start(bq[:, :], bqkv).then_inc(s_w, 16)
            sp.dma_start(kb[0:2, :], tok_kernel).then_inc(s_w, 16)
            sp.dma_start(kb[2:3, :], tok_bias).then_inc(s_w, 16)
            sp.dma_start(bo[:, :], bout).then_inc(s_w, 16)
            sp.dma_start(wo[:, :, :], wout.rearrange("(k p) n -> p k n", p=P)).then_inc(s_w, 16)
            sp.dma_start(sb_member[:, :, :], member.rearrange("p (n j) -> p n j", n=TILES)).then_inc(s_w, 16)
            load_text(0)

            def store_path(b, k):
                sp.wait_ge(S["out_ready"], past(2 * (C9 * b + k) + 2))
                rows = out[ds(b, 1), 2048 * (k // 4):2048 * (k // 4) + 2048, :].rearrange(
                    "o (p n) c -> p (o n) c", n=16)
                sp.dma_start(rows[:, 4 * (k % 4):4 * (k % 4) + 4, :], out_sb[:, k % 2, :, :]).then_inc(
                    S[f"out_stored{k % 2}"], 16)

            def stores(b):
                for k in range(CH):
                    store_path(b, k)
                sp.wait_ge(S["out_ready"], past(2 * (C9 * b + CH) + 2))
                sp.dma_start(out[ds(b, 1), NG:NG + NX, :].rearrange("o p c -> p (o c)"),
                             out_sb[:, 0, 0, :]).then_inc(S["out_stored0"], 16)

            with sp.Fori(0, NB - 1) as b:
                load_points(b + 1)
                load_text(b + 1)
                stores(b)
            sp.wait_ge(S["z_ready"], NB)
            for half in range(2):
                w1b_v = w1b.rearrange("(e r) f -> r e f", e=E)
                sp.dma_start(w1b_z[64 * half:64 * half + 64, half:E:2, :], w1b_v[:, half:E:2, :]).then_inc(S["f_in"], 16)
            sp.dma_start(w1a_s, w1a_t.rearrange("(k p) n -> p k n", p=P)).then_inc(S["f_in"], 16)
            sp.dma_start(w2a_s, w2a_t.rearrange("(k p) n -> p k n", p=P)).then_inc(S["f_in"], 16)
            sp.dma_start(w2b_s, w2b.rearrange("(k p) n -> p k n", p=P)).then_inc(S["f_in"], 16)
            sp.dma_start(ew_s[:, :, :], ew.rearrange("p (n k) -> p n k", k=2)).then_inc(S["f_e"], 16)
            sp.dma_start(ei_s[:, :, :], ei.rearrange("p (n k) -> p n k", k=2)).then_inc(S["f_e"], 16)
            sp.wait_ge(S["out_stored0"], past(16 * 5))
            sp.wait_ge(S["out_stored1"], past(16 * 4))
            ffn_rows = out[0:1, 0:FFN_T, :].rearrange("o (p n) c -> p (o n) c", n=FT)
            sp.dma_start(x1, ffn_rows).then_inc(S["f_x"], 16)
            stores(NB - 1)
            sp.wait_ge(S["out_stored0"], past(16 * 5 * NB))
            sp.wait_ge(S["out_stored1"], past(16 * 4 * NB))
            with sp.Fori(0, FT // 4) as c:
                sp.wait_ge(S["f_out"], 2 * c + 2)
                sp.dma_start(ffn_rows[:, ds(4 * c, 4), :], out_sb[:, 0, :, :]).then_inc(S["f_stored"], 16)
            sp.wait_ge(S["f_stored"], past(16 * (FT // 4)))

        @block.gpsimd
        def _(pool):
            ANGLE_STEPS = 7
            POOL_STEPS = 2 * ANGLE_STEPS + 1 + 24 + 7
            count, base = [0], [0]

            def waiting():
                pool.tensor_tensor(waiter[:, :], eps_col[:, :], eps_col[:, :], ALU.mult)

            for t in (cf[:, :, :], tc, mt[:, :, :], xbd, m3z[:, :, :], z_bd[:, :, :], kt4[:, :, :], v4x[:, :, :]):
                pool.memset(t, 0.0).then_inc(s_zero, 1)
            pool.memset(eps_col[:, :], EPS).then_inc(s_zero, 1)
            pool.memset(halfpi[:, :], math.pi / 2).then_inc(s_zero, 1)
            pool.memset(ones_row[:, :], 1.0).then_inc(s_zero, 1)
            pool.memset(mean_w[:, :], 1.0 / D).then_inc(s_zero, 1)
            pool.wait_ge(s_zero, 12)
            pool.memset(cf[:, :, 3:4], 1.0).then_inc(s_zero, 1)
            pool.memset(tc[:, :, ONEROW:ONEROW + 1], 1.0).then_inc(s_zero, 1)
            def step(ins, scalar=False):
                count[0] += 1
                ins.then_inc(pool_step, 1)
                pool.wait_ge(pool_step, base[0] + count[0])
                if scalar:
                    waiting()

            def tokens(b):
                base[0], count[0] = ANGLE_STEPS + POOL_STEPS * (b - 1), 0
                pool.wait_ge(S["sin_ready"], 4 * b)
                pool.wait_ge(s_xin, 32 * b + 32)
                for i in range(2):
                    angles(pool, step, i, rnd)
                products(pool, step, b, waiting)
                assert count[0] == POOL_STEPS, count[0]

            def spread(b, k):
                c = C9 * b + k
                pool.wait_ge(S["rd_ready"], c + 1)
                pool.wait_ge(S["rdt_ps"], past(2 * c))
                waiting()
                pool.tensor_scalar(rd_all[:, :, :, :],
                                   rd[:, :, :].rearrange("p n (h o) -> p n h o", o=1).to_broadcast([P, 4, H, DH]),
                                   1.0, 0.0, ALU.mult, ALU.add).then_inc(S["rdb_ready"], 1)

            def batch(b, last):
                if not last:
                    tokens(b + 1)
                if last:
                    pool.wait_ge(S["z_ready"], NB)
                    for half in range(2):
                        pool.memset(w1b_z[64 - 64 * half:128 - 64 * half, half:E:2, :], 0.0).then_inc(S["f_zero"], 1)
                        pool.wait_ge(S["f_zero"], half + 1)
                    pool.memset(wt, 0.0).then_inc(S["f_zero"], 1)
                with pool.Fori(0, C9) as k:
                    spread(b, k)

            pool.wait_ge(s_const, 16)
            pool.wait_ge(s_xin, 32)
            angles(pool, step, 1, rnd)
            with pool.Fori(0, NB - 1) as b:
                batch(b, False)
            batch(NB - 1, True)

        @block.scalar
        def _(act):
            def sines(b):
                act.wait_ge(S["ang0_ready"], b + 1)
                if not first(b):
                    act.wait_ge(S["var_ready"], b)
                act.activation(sin_a[:, :, :], ang[0][:, :, :], ACT.Sin, scale=0.5).then_inc(S["sin_ready"], 1)
                act.activation(abs_a[:, :, :], ang[0][:, :, :], ACT.Abs, scale=0.5).then_inc(S["sin_ready"], 1)
                act.wait_ge(S["sin_ready"], 4 * b + 2)
                act.activation(re[:, :, :], abs_a[:, :, :], ACT.Sin, bias=halfpi[:, :], scale=-1.0).then_inc(
                    S["sin_ready"], 1)
                act.wait_ge(S["ang1_ready"], b + 1)
                act.activation(im[:, :, :], ang[1][:, :, :], ACT.Sin, scale=2.0).then_inc(S["sin_ready"], 1)

            def deviations(b):
                act.wait_ge(S["var_ready"], b + 1)
                act.activation(sd[:, :], st[:, 3, :], ACT.Sqrt, bias=eps_col[:, :]).then_inc(S["sd_ready"], 1)
                act.wait_ge(S["txvar_ready"], b + 1)
                act.activation(txsd[:, 0:1], txmv[:, 1:2], ACT.Sqrt, bias=eps_col[:, :]).then_inc(S["sd_ready"], 1)

            def setup_sequence(b):
                for i in range(5):
                    act.wait_ge(S["coef_ps"], C9 * b + 2 * i + 1)
                    w = 512 if i < 4 else P
                    act.activation(coef_t[:, 1024 * i:1024 * i + w], psb(COEF_BANKS[2 * i % 4])[:, 0:w], ACT.Copy).then_inc(
                        S["coef_act"], 1)
                act.wait_ge(S["qkx_ps"], b + 1)
                act.activation(qkv_x[:, 512:768], ps[:, 4, 0:256], ACT.Copy).then_inc(S["qkx_sb"], 1)
                act.wait_ge(S["s2_sub"], b + 1)
                act.activation(s2[:, :, :], s2[:, :, :], ACT.Exp).then_inc(S["s2_exp"], 1)
                for i, (g, bank, half) in enumerate(G_ORDER):
                    act.wait_ge(S["g_ps"], 4 * b + i + 1)
                    for r in (slice(0, 32), slice(64, 128)):
                        ins = act.activation(g[r, 512 * half:512 * half + 512], ps[r, bank, :], ACT.Copy)
                    ins.then_inc(S["g_first"], 1)
                for i in range(2):
                    act.wait_ge(S["xt_ps"], 2 * b + i + 1)
                    act.activation(xt[:, 4 * i:4 * i + 4, :], ps[:, i, :].rearrange("p (n c) -> p n c", n=4),
                                   ACT.Copy).then_inc(S["xt_sb"], 1)

            def exp3(b, n):
                if n == 0 and not first(b):
                    act.wait_ge(S["ud_pe"], past(2 * C9 * b))
                if n >= 4 and n % 2 == 0:
                    act.wait_ge(S["pv3_pe"], 17 * b + n // 2 - 1)
                for i in range(2):
                    act.wait_ge(S[f"s3_pe{i}"], TILES * b + n + 1)
                    act.activation(p3[:, n % 4, 512 * i:512 * i + 512], ps[:, 6 + i, :], ACT.Exp).then_inc(
                        S[f"s3_exp{i}"], 1)

            def pseudo_inverse(b):
                pe, done = [0, 0], [0, 0]
                for s, k, half, within, after in pinv_steps():
                    rows = slice(4 * half, 4 * half + 4)

                    def exps(fill):
                        for kind, n in fill:
                            if kind == "tile":
                                exp3(b, n)

                    def copy(dst, i, scale):
                        act.activation(dst[:, rows, :], pinv_bank(half, i), ACT.Copy, scale=scale).then_inc(
                            S[f"pi_act{half}"], 1)
                        done[half] += 1

                    exps(sum(within, []))
                    pe[half] += 1
                    act.wait_ge(S[f"pi_pe{half}"], PI_PE * b + pe[half])
                    if s == "init":
                        copy(ym, 0, 1.0)
                        copy(yt, 1, 1.0)
                    elif s == "square":
                        copy(y2t, 0, 1.0)
                    elif s == "next" and k < ITERS - 1:
                        copy(ym, 0, 0.25)
                        copy(yt, 1, 0.25)
                        copy(vt, 2, 0.25)
                    elif s == "next":
                        copy(vt, 2, 0.25)
                    exps(after)
                assert done[0] == PI_ACT and pe[0] == PI_PE

            def group(b, k, g, pp, w):
                c = C9 * b + k
                if pp == 0:
                    if first(k):
                        act.wait_ge(S["o3_ps"], b + 1)
                    elif not first(c):
                        act.wait_ge(S["ud_pe"], past(2 * c + g - 1))
                act.wait_ge(S["s1_pe"], 8 * c + 4 * g + pp + 1)
                act.activation(p1[:, g, pp, 0:w], ps[:, 2 + pp % 2, 0:w], ACT.Exp).then_inc(S["p1_ready"], 1)

            def u_copy(b, k, g, par, w):
                c = C9 * b + k
                act.wait_ge(S["ud_pe"], past(2 * c + g + 1))
                act.activation(u_sb[:, par, g, 0:w], ps[:, 4, 0:w], ACT.Copy).then_inc(S["u_ready"], 1)

            def out_copy(b, kp, par):
                cp = C9 * b + kp
                act.wait_ge(S["out_ps"], past(2 * cp + 2))
                act.activation(out_sb[:, par, 2:4, :], ps[:, 6, :].rearrange("p (n c) -> p n c", n=2),
                               ACT.Copy).then_inc(S["out_ready"], 1)

            def chunk(b, k, par, w, before):
                for pp in range(4):
                    group(b, k, 0, pp, w)
                group(b, k, 1, 0, w)
                u_copy(b, k, 0, par, w)
                if before:
                    out_copy(b, k - 2, par)
                for pp in range(1, 4):
                    group(b, k, 1, pp, w)
                u_copy(b, k, 1, par, w)

            def batch(b, last):
                setup_sequence(b)
                if not last:
                    sines(b + 1)
                pseudo_inverse(b)
                if not last:
                    deviations(b + 1)
                chunk(b, 0, 0, 512, False)
                chunk(b, 1, 1, 512, False)
                with act.Fori(1, CH // 2 - 1) as i:
                    chunk(b, 2 * i, 0, 512, True)
                    chunk(b, 2 * i + 1, 1, 512, True)
                chunk(b, CH - 2, 0, 512, True)
                chunk(b, CH - 1, 1, 512, True)
                chunk(b, CH, 0, P, True)
                out_copy(b, CH - 1, 1)

            act.wait_ge(s_zero, 14)
            sines(0)
            deviations(0)
            with act.Fori(0, NB - 1) as b:
                batch(b, False)
            batch(NB - 1, True)

            act.wait_ge(S["f_var"], 1)
            act.activation(fsd[:, 0, :], fmv[:, :, 1], ACT.Sqrt, bias=eps_col[:, :]).then_inc(S["f_sd"], 1)
            with act.Fori(0, FT // 4) as c:
                for p in range(E // 2):
                    for f in range(FB):
                        u = (4 * c + p) * FB + f
                        for e in range(2):
                            act.wait_ge(S["f_l1"], 2 * u + e + 1)
                            act.activation(hid[:, e, f % 2, :], ps[:, 2 * (f % 2) + e, :], ACT.Gelu).then_inc(
                                S["f_gelu"], 1)

        @block.vector
        def _(dve):
            count = [0]
            base = [0]

            def step(ins, scalar=False):
                count[0] += 1
                ins.then_inc(dve_step, 1)
                dve.wait_ge(dve_step, base[0] + count[0])

            def split(dst, src, width):
                r = split_r[64:128, 0:width]
                dve.tensor_copy(dst[0:32], src[0:32])
                step(dve.tensor_copy(dst[64:128], src[64:128]))
                return lower_parts(dst, src, width)

            def lower_parts(dst, src, width):
                r = split_r[64:128, 0:width]
                step(dve.tensor_tensor(r, src[64:128], dst[64:128], ALU.subtract))
                step(dve.tensor_copy(dst[64:128], r))
                return dve.tensor_tensor(dst[96:128], split_r[96:128, 0:width], dst[96:128], ALU.subtract)

            def split_g(b, i):
                g, bank, half = G_ORDER[i]
                dve.wait_ge(S["g_first"], 4 * b + i + 1)
                if i:
                    dve.wait_ge(S["g_ready"], 4 * b + i)
                lower_parts(g[:, 512 * half:512 * half + 512], ps[:, bank, :], 512).then_inc(S["g_ready"], 1)

            for i, name in enumerate(FROM_ONE):
                dve.memset(started[:, i:i + 1], 0.0).then_inc(S[name], 1)

            dve.wait_ge(s_const, 16)
            dve.wait_ge(s_xin, 32)
            angles(dve, step, 0, (re, im))

            dve.wait_ge(s_w, 16 * 7)
            dve.wait_ge(s_zero, 14)
            dve.tensor_copy(identb[:, :], ident)
            dve.tensor_copy(g1[32:64, :], con("negind")[32:64])
            dve.tensor_scalar(id7[:, :], ident, 7.0, None, ALU.mult)
            dve.tensor_scalar(id13[:, :], ident, 13.0, None, ALU.mult)
            dve.tensor_scalar(wq[:, :, 0:D], wq[:, :, 0:D], DH ** -0.5, None, ALU.mult)
            dve.tensor_scalar(bq[:, 0:D], bq[:, 0:D], DH ** -0.5, None, ALU.mult)
            step(dve.tensor_reduce(ksum[:, 0:1], kb[:, :], AX.X, ALU.add))
            step(dve.tensor_scalar(ksum[:, 1:2], ksum[:, 0:1], 1.0 / D, None, ALU.mult))
            dve.tensor_scalar(kbc[:, :], kb[:, :], ksum[:, 1:2], None, ALU.subtract).then_inc(S["kbc_ready"], 1)
            dve.wait_ge(S["kt_ps"], 1)
            step(dve.tensor_copy(kt4[:, :, 0:3], ps[:, 0, 0:8].rearrange("p (k c) -> p k c", k=2)[:, :, 0:3]))
            dve.tensor_tensor(prod[:, :, 0:3], kt4[:, :, 0:3], kt4[:, :, 0:3], ALU.mult)
            dve.tensor_tensor(prod[:, :, 3:5], kt4[:, :, 0:2], kt4[:, :, 1:3], ALU.mult)
            dve.tensor_tensor(prod[:, :, 5:6], kt4[:, :, 0:1], kt4[:, :, 2:3], ALU.mult).then_inc(S["kt4_ready"], 1)
            dve.wait_ge(S["gram_ps"], 1)
            dve.tensor_copy(gram[:, 0:3], ps[:, 1, 0:3])
            dve.tensor_scalar(gram[:, 3:6], ps[:, 1, 3:6], 2.0, None, ALU.mult).then_inc(S["gram_sb"], 1)
            PER = 23

            def text_stats(b):
                dve.wait_ge(s_txin, 16 * b + 16)
                step(dve.bn_stats(txstat[:, :], tx[:, :]))

            def text_variance():
                dve.bn_aggr(txmv[:, :], txstat[:, :]).then_inc(S["txvar_ready"], 1)

            def text_rows(b):
                dve.wait_ge(S["sd_ready"], 2 * b + 2)
                step(dve.reciprocal(txsd[:, 1:2], txsd[:, 0:1]))
                dve.tensor_scalar(txn[:, :], tx[:, :], txmv[:, 0:1], txsd[:, 1:2], ALU.subtract, ALU.mult).then_inc(
                    S["txn_ready"], 1)

            def coefficients():
                step(dve.reciprocal(rstd[:, :], sd[:, :]))
                rb = rstd[:, :].rearrange("p (n o) -> p n o", o=1)
                dve.tensor_copy(cf[:, 0:NT, 2:3], rb)
                step(dve.tensor_tensor(cf[:, 0:NT, 0:2], reim[:, :, :], rb.to_broadcast([P, NT, 2]), ALU.mult))

            def parts(src, tmp, n, cols):
                t = tc[:, 0:NT, :]
                for c in cols[1][1:]:
                    dve.tensor_copy(t[:, :, c:c + n], src)
                c = cols[1][0]
                step(dve.tensor_copy(t[:, :, c:c + n], src))
                step(dve.tensor_tensor(tmp, src, t[:, :, c:c + n], ALU.subtract))
                for c in cols[2][1:]:
                    dve.tensor_copy(t[:, :, c:c + n], tmp)
                c = cols[2][0]
                step(dve.tensor_copy(t[:, :, c:c + n], tmp))
                c3_ = cols[3][0]
                return dve.tensor_tensor(t[:, :, c3_:c3_ + n], tmp, t[:, :, c:c + n], ALU.subtract)

            def landmark_coefficient_parts():
                step(parts(cf[:, 0:NT, 0:4], ce[:, :, :], 4, A_COLS))

            def residual_coefficient_parts():
                parts(reim[:, :, :], ce[:, :, 0:2], 2, B_COLS).then_inc(S["tc_ready"], 1)

            def setup_sequence(b):
                dve.memset(g3[32:64, :], 0.0)
                dve.wait_ge(S["txnt_ps"], b + 1)
                dve.tensor_copy(txn_t[:, :, :], ps[:, 2, 0:256].rearrange("p (k c) -> p k c", k=2)).then_inc(
                    S["txnt_sb"], 1)
                dve.tensor_tensor(txr[:, :], tx[:, :], bout_all[:, :], ALU.add).then_inc(S["tx_used"], 1)
                for i in range(4):
                    dve.wait_ge(S["coef_ps"], C9 * b + 2 * i + 2)
                    dve.tensor_copy(coef_t[:, 1024 * i + 512:1024 * i + 1024], psb(COEF_BANKS[(2 * i + 1) % 4])[:, 0:512]).then_inc(
                        S["coef_dve"], 1)
                dve.wait_ge(S["qkx_ps"], b + 1)
                dve.tensor_tensor(qkv_x[:, 0:512], ps[:, 3, :], bq_all[:, :], ALU.add).then_inc(S["qkx_bias"], 1)
                dve.wait_ge(S["lm_ps"], b + 1)
                dve.tensor_copy(lm_c[:, :], ps[0:4, 6, 0:LM]).then_inc(S["lm_sb"], 1)
                dve.wait_ge(S["qkxt_ps"], b + 1)
                dve.tensor_copy(qk_xt[:, :, :], ps[:, 5, :].rearrange("p (n c) -> p n c", n=4)).then_inc(
                    S["qkxt_sb"], 1)
                dve.wait_ge(S["qkl_ps"], b + 1)
                qkl = ps[:, 2, 0:256].rearrange("p (n o j) -> p n o j", n=4, o=1)
                mask = con("mask8").rearrange("p (h o) -> p h o", o=1).to_broadcast([P, 8, LM])
                dve.tensor_copy(klt[:, :, :], qkl[:, 2:4, 0, :])
                for t, part in ((ql_bd, 0), (kl_bd, 2)):
                    for half in range(2):
                        ins = dve.tensor_tensor(t[:, half, :, :], qkl[:, part + half, :, :].to_broadcast([P, 8, LM]),
                                                mask, ALU.mult)
                    ins.then_inc(S["klbd_ready" if part else "qlbd_ready"], 1)
                dve.wait_ge(S["s2_ps"], b + 1)
                s2_ps = ps[:, 4, :].rearrange("p (n c) -> p n c", n=PAIRS)
                step(dve.tensor_reduce(s2m[:, 0, :], s2_ps, AX.X, ALU.max))
                dve.tensor_tensor(s2[:, :, :], s2_ps,
                                  s2m[:, 0, :].rearrange("p (n o) -> p n o", o=1).to_broadcast([P, PAIRS, LM]),
                                  ALU.subtract).then_inc(S["s2_sub"], 1)
                dve.wait_ge(S["s2_exp"], b + 1)
                step(dve.tensor_reduce(s2m[:, 0, :], s2[:, :, :], AX.X, ALU.add))
                step(dve.reciprocal(s2m[:, 1, :], s2m[:, 0, :]))
                for i in range(2):
                    r = slice(64 * i, 64 * i + 64)
                    ins = dve.tensor_tensor(
                        xbd[r, :, 64 * i:64 * i + 64], s2[r, :, :],
                        s2m[r, 1, :].rearrange("p (n o) -> p n o", o=1).to_broadcast([64, PAIRS, LM]), ALU.mult)
                ins.then_inc(S["xbd_ready"], 1)
                for i in range(4):
                    split_g(b, i)

            def pseudo_inverse(b):
                pe, act_n = [0, 0], [0, 0]

                def maxima(b, u):
                    p, k = UNITS[u]
                    dve.wait_ge(S["s3m_pe"], len(UNITS) * b + u + 1)
                    bank = ps[:, 6 + u % 2, :]
                    if p is None:
                        dve.tensor_reduce(m3part[:, 4 * k:4 * k + 4, CH], bank.rearrange("p (n c) -> p n c", n=4),
                                          AX.X, ALU.max).then_inc(S["s3m_used"], 1)
                    else:
                        dve.tensor_reduce(m3part[:, p, k:k + 1], bank, AX.X, ALU.max).then_inc(S["s3m_used"], 1)

                for s, k, half, within, after in pinv_steps():
                    rows = slice(4 * half, 4 * half + 4)
                    for kind, what in sum(within, []):
                        if kind == "unit":
                            maxima(b, what)

                    def eye(t):
                        return t[:, :].rearrange("p (o c) -> p o c", o=1).to_broadcast([P, 4, P])

                    pe[half] += 1
                    if s == "init" or (s == "next" and k < ITERS - 1):
                        dve.wait_ge(S[f"pi_act{half}"], past(PI_ACT * b + act_n[half] + 1))
                        act_n[half] += 2 if s == "init" else 3
                        dve.scalar_tensor_tensor(out=y7[:, rows, :], in0=ym[:, rows, :], scalar=-1.0, in1=eye(id7),
                                                 op0=ALU.mult, op1=ALU.add)
                        dve.scalar_tensor_tensor(out=ylin[:, rows, :], in0=ym[:, rows, :], scalar=-15.0,
                                                 in1=eye(id13), op0=ALU.mult, op1=ALU.add).then_inc(
                            S[f"pi_dve{half}"], 1)
                    elif s == "square":
                        act_n[half] += 1
                    elif s == "poly":
                        dve.wait_ge(S[f"pi_pe{half}"], PI_PE * b + pe[half])
                        dve.wait_ge(S[f"pi_dve{half}"], past(PI_DVE * b + 2 * k + 1))
                        dve.tensor_tensor(qm[:, rows, :], pinv_bank(half, 1), ylin[:, rows, :], ALU.add).then_inc(
                            S[f"pi_dve{half}"], 1)
                    for kind, what in after:
                        if kind == "unit":
                            maxima(b, what)
                        elif kind == "row":
                            row_max(b, 0, what, False)
                        elif kind == "max":
                            dve.wait_ge(S["s3m_used"], len(UNITS) * (b + 1))
                            dve.tensor_reduce(m3z[:, :, 16:17], m3part[:, :, :], AX.X, ALU.max).then_inc(
                                S["m3_ready"], 1)
                        elif kind == "shift":
                            dve.wait_ge(S["m3_ps"], b + 1)
                            dve.tensor_scalar(g3[32:64, :], ps[32:64, 6:8, :].rearrange("p a c -> p (a c)"), -1.0,
                                              None, ALU.mult).then_inc(S["g3_shift"], 1)

            def landmark_values(b, last):
                dve.wait_ge(S["pv3_pe"], 17 * (b + 1))
                dve.tensor_copy(c3[:, :], ps[:, 5, :]).then_inc(S["c3_sb"], 1)
                if not last:
                    text_variance()
                dve.wait_ge(S["o3_ps"], b + 1)
                o3 = ps[:, 4, 0:272].rearrange("p (n c) -> p n c", n=PAIRS)
                step(dve.reciprocal(w3r[:, :], o3[:, :, 32]))
                for i in range(2):
                    r = slice(64 * i, 64 * i + 64)
                    ins = dve.tensor_tensor(
                        w3[r, :, :], o3[r, :, 16 * i:16 * i + 16],
                        w3r[r, :].rearrange("p (n o) -> p n o", o=1).to_broadcast([64, PAIRS, DH]), ALU.mult)
                ins.then_inc(S["w3_ready"], 1)
                max_rows(b, 0, 512)
                dve.wait_ge(S["z_ps"], b + 1)
                for i in range(2):
                    r = slice(64 * i, 64 * i + 64)
                    ins = dve.tensor_copy(z_bd[r, :, 16 * i:16 * i + 16],
                                          ps[r, 6, 0:128].rearrange("p (n c) -> p n c", n=PAIRS))
                ins.then_inc(S["z_ready"], 1)

            def row_max(b, k, j, text):
                t = 4 * (C9 * b + k) + j
                dve.wait_ge(S["s1m_pe"], t + 1)
                dve.tensor_reduce(m1[:, j, :], ps[:, 0:2, :].rearrange("p a (h c) -> p (a h) c", c=LM), AX.X,
                                  ALU.max).then_inc(S["s1m_used"], 4 if text else 1)

            def max_rows(b, k, w):
                dve.wait_ge(S["m1t_ps"], C9 * b + k + 1)
                dve.tensor_copy(coef_t[MAXROW:MAXROW + H, ds(512 * k, w)], psb(0)[MAXROW:MAXROW + H, 0:w]).then_inc(
                    S["m1t_sb"], 1)

            def denominators(b, kp, w):
                cp = C9 * b + kp
                n = w // P
                dve.wait_ge(S["dt_ps"], past(cp + 1))
                dve.tensor_reduce(d_t[:, 0:n, :], ps[:, 7, 0:w].rearrange("p (n q h) -> p n h q", n=n, q=4)[:, :, 0:H, :],
                                  AX.X, ALU.add).then_inc(S["dt_used"], 1)
                dve.wait_ge(S["dt_used"], cp + 1)
                if not first(cp):
                    dve.wait_ge(S["rdb_ready"], past(cp))
                dve.reciprocal(rd[:, 0:n, :], d_t[:, 0:n, :]).then_inc(S["rd_ready"], 1)

            def normalise(b, kp, g, par, w):
                cp = C9 * b + kp
                dve.wait_ge(S["rdt_ps"], past(2 * cp + g + 1))
                dve.wait_ge(S["u_ready"], past(2 * cp + g + 1))
                if g == 0:
                    dve.wait_ge(S["out_ps"], past(2 * cp))
                dve.tensor_tensor(o_sb[:, g, 0:w], ps[:, 7, 0:w], u_sb[:, par, g, 0:w], ALU.mult).then_inc(
                    S["o_ready"], 1)

            def d_copy(b, k, w):
                dve.wait_ge(S["ud_pe"], past(2 * (C9 * b + k) + 2))
                dve.wait_ge(S["dt_ps"], past(C9 * b + k))
                dve.tensor_copy(d_sb[:, 0:w], ps[:, 5, 0:w]).then_inc(S["d_ready"], 1)

            def out_copy(b, kp, par, i):
                dve.wait_ge(S["out_ps"], past(2 * (C9 * b + kp) + 1))
                dve.wait_ge(S[f"out_stored{par}"], past(16 * ((5 - par) * b + i)))
                dve.tensor_copy(out_sb[:, par, 0:2, :], ps[:, 6, :].rearrange("p (n c) -> p n c", n=2)).then_inc(
                    S["out_ready"], 1)

            def text_out(b):
                cp = C9 * b + CH
                dve.wait_ge(S["out_ps"], past(2 * cp + 1))
                dve.wait_ge(S["out_stored0"], past(16 * (5 * b + 4)))
                dve.tensor_tensor(out_sb[:, 0, 0, :], ps[:, 6, 0:256], txr[:, :], ALU.add).then_inc(S["out_ready"], 2)

            def chunk(b, k, par, w, prev, nxt, i=0, between=None):
                text_next = nxt and isinstance(k, int) and k == CH - 1
                rows = nxt and not text_next
                if prev:
                    denominators(b, k - 1, 512)
                if nxt:
                    row_max(b, k + 1, 0, text_next)
                if prev:
                    normalise(b, k - 1, 0, 1 - par, 512)
                if rows:
                    row_max(b, k + 1, 1, False)
                if prev:
                    normalise(b, k - 1, 1, 1 - par, 512)
                if rows:
                    row_max(b, k + 1, 2, False)
                    row_max(b, k + 1, 3, False)
                d_copy(b, k, w)
                if nxt:
                    max_rows(b, k + 1, P if text_next else 512)
                if between:
                    between()
                if prev:
                    out_copy(b, k - 1, 1 - par, i)

            def expert_weights():
                dve.wait_ge(S["f_e"], 32)
                step(dve.tensor_copy(ei_f[:, :, :], ei_s[:, :, :]))
                for k in range(2):
                    iota = con("iota8").rearrange("p (o e) -> p o e", o=1).to_broadcast([P, FT, E])
                    step(dve.tensor_tensor(eq[:, k, :, :], ei_f[:, :, k:k + 1].to_broadcast([P, FT, E]), iota, ALU.is_equal))
                    step(dve.tensor_tensor(eq[:, k, :, :], eq[:, k, :, :], ew_s[:, :, k:k + 1].to_broadcast([P, FT, E]),
                                           ALU.mult))
                step(dve.tensor_tensor(eq[:, 0, :, :], eq[:, 0, :, :], eq[:, 1, :, :], ALU.add))
                dve.tensor_copy(sel_e, con("selE"))
                dve.wait_ge(S["f_zero"], 3)
                w1, w2, w3_ = (wt[:, :, a:a + E] for a in WEIGHT_ROWS)
                step(dve.tensor_copy(w1, eq[:, 0, :, :]))
                step(dve.tensor_tensor(eq[:, 1, :, :], eq[:, 0, :, :], w1, ALU.subtract))
                step(dve.tensor_copy(w2, eq[:, 1, :, :]))
                dve.tensor_tensor(w3_, eq[:, 1, :, :], w2, ALU.subtract).then_inc(S["f_we"], 1)

            def row_statistics(half):
                if half == 0:
                    dve.wait_ge(S["f_x"], 16)
                for n in range(8 * half, 8 * half + 8):
                    ins = dve.bn_stats(fst[:, n, :], x1[:, n, :])
                step(ins)
                if half == 1:
                    for n in range(FT):
                        ins = dve.bn_aggr(fmv[:, n, :], fst[:, n, :])
                    ins.then_inc(S["f_var"], 1)

            def batch(b, last):
                count[0] = 0
                base[0] = SETUP + PER * b
                setup_sequence(b)
                pseudo_inverse(b)
                if not last:
                    text_stats(b + 1)
                landmark_values(b, last)
                chunk(b, 0, 0, 512, False, True, 0, None if last else (lambda: text_rows(b + 1)))
                chunk(b, 1, 1, 512, True, True, 0, None if last else coefficients)
                with dve.Fori(1, CH // 2 - 1) as i:
                    chunk(b, 2 * i, 0, 512, True, True, i - 1)
                    chunk(b, 2 * i + 1, 1, 512, True, True, i)
                chunk(b, CH - 2, 0, 512, True, True, 2, expert_weights if last else landmark_coefficient_parts)
                chunk(b, CH - 1, 1, 512, True, True, 3, (lambda: row_statistics(0)) if last else residual_coefficient_parts)
                chunk(b, CH, 0, P, True, False, 3, (lambda: row_statistics(1)) if last else None)
                denominators(b, CH, P)
                normalise(b, CH, 0, 0, P)
                normalise(b, CH, 1, 0, P)
                text_out(b)
                assert last or count[0] == PER, count[0]

            dve.wait_ge(S["gram_sb"], 1)
            products(dve, step, 0, lambda: None)
            dve.wait_ge(S["m4_ps"], 1)
            dve.tensor_copy(m4[:, 0:512], ps[0:4, 2, :])
            dve.tensor_copy(m4[:, 512:768], ps[0:4, 3, 0:256]).then_inc(S["m4_sb"], 1)
            text_stats(0)
            text_variance()
            text_rows(0)
            coefficients()
            landmark_coefficient_parts()
            residual_coefficient_parts()

            dve.wait_ge(S["mt_ps"], 1)
            for n in (1, 2, 3):
                for col in A_COLS[n]:
                    dve.tensor_copy(mt[:, :, col:col + 4], ps[:, 4, 0:16].rearrange("p (n c) -> p n c", n=4))
            dve.wait_ge(S["v4_ps"], 1)
            for half in range(2):
                dve.tensor_copy(v4x[:, 4 * half:4 * half + 4, 0:32],
                                ps[:, 5, 128 * half:128 * half + 128].rearrange("p (n c) -> p n c", n=4))
                dve.tensor_copy(v4x[:, 4 * half:4 * half + 4, 32:33],
                                con("col32")[:, half:half + 1].rearrange("p (a b) -> p a b", a=1).to_broadcast([P, 4, 1]))
            dve.wait_ge(S["bout_ps"], 1)
            dve.tensor_copy(bout_all[:, :], ps[:, 7, 0:256])
            dve.tensor_copy(bq_all[:, :], ps[:, 3, :])
            dve.memset(res_w[32:64, :], 0.0)
            split(res_w, ps[:, 6, 0:256], D).then_inc(S["setup_sb"], 1)
            SETUP = count[0]
            with dve.Fori(0, NB - 1) as b:
                batch(b, False)
            batch(NB - 1, True)

            dve.wait_ge(S["f_sd"], 1)
            step(dve.reciprocal(fsd[:, 1, :], fsd[:, 0, :]))

            def normalise_rows(c):
                if not first(c):
                    dve.wait_ge(S["f_xnt_ps"], 2 * c)
                for j in range(4):
                    ins = dve.tensor_scalar(xn[:, j, :], x1[:, ds(4 * c + j, 1), :].rearrange("p o c -> p (o c)"),
                                            fmv[:, ds(4 * c + j, 1), 0:1].rearrange("p a b -> p (a b)"),
                                            fsd[:, 1, ds(4 * c + j, 1)], ALU.subtract, ALU.mult)
                ins.then_inc(S["f_xn"], 1)

            def turned_rows(c):
                for i in range(2):
                    dve.wait_ge(S["f_xnt_ps"], 2 * c + i + 1)
                    dve.tensor_copy(xn_t[:, :, 256 * i:256 * i + 256],
                                    ps[:, 6 + i, :].rearrange("p (k c) -> p k c", k=2)).then_inc(S["f_xnt"], 1)

            def out_rows(c):
                for i in range(2):
                    dve.wait_ge(S["f_out_ps"], 2 * c + i + 1)
                    if i == 0:
                        dve.wait_ge(S["f_stored"], past(16 * c))
                    dve.tensor_tensor(out_sb[:, 0, 2 * i:2 * i + 2, :], ps[:, 6 + i, :].rearrange("p (n c) -> p n c", n=2),
                                      x1[:, ds(4 * c + 2 * i, 2), :], ALU.add).then_inc(S["f_out"], 1)

            def experts(c, last):
                for p in range(E // 2):
                    dve.wait_ge(S["f_l0"], 4 * c + p + 1)
                    dve.tensor_copy(mid[:, p, :], ps[:, 4 + p % 2, :]).then_inc(S["f_mid"], 1)
                if not first(c):
                    out_rows(c - 1)
                for p in range(E // 2):
                    if p == 1 and not last:
                        normalise_rows(c + 1)
                    dve.wait_ge(S["f_wx_ps"], 4 * c + p + 1)
                    if not (first(c) and p == 0):
                        dve.wait_ge(S["f_y2"], 4 * c + p)
                    dve.tensor_copy(wx[:, :], ps[:, 6, :]).then_inc(S["f_wx"], 1)
                    if p == 2 and not last:
                        turned_rows(c + 1)
                    dve.wait_ge(S["f_wx"], 4 * c + p + 1)
                    dve.wait_ge(S["f_l2"], FB * (4 * c + p + 1))
                    dve.tensor_tensor(y2[:, p, :], ps[:, 4 + p % 2, :], wx[:, :], ALU.mult).then_inc(S["f_y2"], 1)

            normalise_rows(0)
            dve.wait_ge(S["out_stored0"], past(16 * 5 * NB))
            for i in range(4):
                dve.wait_ge(S["f_wet_ps"], i + 1)
                dve.tensor_copy(we_t[:, 512 * i:512 * i + 512], psb(i)[:, 0:512]).then_inc(S["f_wet"], 1)
            turned_rows(0)
            experts(0, False)
            with dve.Fori(1, FT // 4 - 1) as c:
                experts(c, False)
            experts(FT // 4 - 1, True)
            out_rows(FT // 4 - 1)

        @block.tensor
        def _(pe):
            pe.wait_ge(S["kbc_ready"], 1)
            for k in range(2):
                ins = pe.transpose(ps[:, 0, 4 * k:4 * k + 3], kbc[:, 128 * k:128 * k + 128], ident[0:3, 0:3])
            ins.then_inc(S["kt_ps"], 1)
            pe.wait_ge(S["kt4_ready"], 1)
            for k in range(2):
                ins = pe.matmul(ps[:, 1, 0:6], mean_w[:, :], prod[:, k, :], start=k == 0, stop=k == 1)
            ins.then_inc(S["gram_ps"], 1)
            e3 = con("e3")[0:1, :]
            for i, (a, n) in enumerate(((0, 512), (512, 256))):
                for k in range(2):
                    pe.matmul(ps[0:4, 2 + i, 0:n], kt4[:, k, :], wq[:, k, a:a + n], start=k == 0, stop=False)
                ins = pe.matmul(ps[0:4, 2 + i, 0:n], e3, bq[:, a:a + n], start=False, stop=True)
            ins.then_inc(S["m4_ps"], 1)
            for n in range(4):
                o = ps[:, 4, 4 * n:4 * n + 4]
                for k in range(2):
                    pe.matmul(o, wq[:, k, 128 * n:128 * n + 128], kt4[:, k, :], start=k == 0, stop=False)
                ins = pe.matmul(o, bq[:, 128 * n:128 * n + 128], e3, start=False, stop=True)
            ins.then_inc(S["mt_ps"], 1)
            pe.wait_ge(S["m4_sb"], 1)
            for half in range(2):
                ins = pe.matmul(ps[:, 5, 128 * half:128 * half + 128],
                                con("selV")[0:4, 128 * half:128 * half + 128],
                                m4[:, 512 + 128 * half:640 + 128 * half], start=True, stop=True)
            ins.then_inc(S["v4_ps"], 1)
            pe.matmul(ps[:, 6, 0:256], con("sel3")[0:3, :], kb[:, :], start=True, stop=False)
            pe.matmul(ps[:, 6, 0:256], con("sel1")[0:1, :], bo[:, :], start=False, stop=True)
            pe.matmul(ps[:, 3, :], ones_row[:, :], bq[:, 0:512], start=True, stop=True)
            pe.matmul(ps[:, 7, 0:256], ones_row[:, :], bo[:, :], start=True, stop=True).then_inc(S["bout_ps"], 1)

            def setup_sequence(b):
                pe.wait_ge(S["txn_ready"], b + 1)
                for k in range(2):
                    ins = pe.transpose(ps[:, 2, 128 * k:128 * k + 128], txn[:, 128 * k:128 * k + 128], ident)
                ins.then_inc(S["txnt_ps"], 1)
                pe.wait_ge(S["tc_ready"], b + 1)

                def text_qkv():
                    pe.wait_ge(S["setup_sb"], 1)
                    pe.wait_ge(S["txnt_sb"], b + 1)
                    for i, (a, n) in enumerate(((0, 512), (512, 256))):
                        for k in range(2):
                            ins = pe.matmul(ps[:, 3 + i, 0:n], txn_t[:, k, :], wq[:, k, a:a + n], start=k == 0,
                                            stop=k == 1)
                    ins.then_inc(S["qkx_ps"], 1)

                for i in range(C9):
                    if i == 2:
                        text_qkv()
                    if i >= 4:
                        done = ("coef_dve", 4 * b) if i % 2 else ("coef_act", 5 * b)
                        pe.wait_ge(S[done[0]], done[1] + i // 2 - 1)
                    for j in range(4 if i < CH else 1):
                        ins = pe.transpose(psb(COEF_BANKS[i % 4])[:, 128 * j:128 * j + 128], tc[:, 4 * i + j, :], identb[:, :])
                    ins.then_inc(S["coef_ps"], 1)
                pe.wait_ge(S["coef_act"], 5 * b + 4)
                for n in range(NT):
                    ins = pe.matmul(ps[0:32, 6, 0:LM], cf[:, n, :], sb_member[:, n, :], start=n == 0, stop=n == NT - 1)
                ins.then_inc(S["lm_ps"], 1)
                pe.wait_ge(S["qkx_sb"], b + 1)
                pe.wait_ge(S["qkx_bias"], b + 1)
                for n in range(4):
                    ins = pe.transpose(ps[:, 5, 128 * n:128 * n + 128], qkv_x[:, 128 * n:128 * n + 128], ident)
                ins.then_inc(S["qkxt_ps"], 1)
                pe.wait_ge(S["lm_sb"], b + 1)
                for n in range(4):
                    o = ps[:, 2, LM * n:LM * n + LM]
                    pe.matmul(o, m4[:, 128 * n:128 * n + 128], lm_c[:, :], start=True, stop=False)
                    ins = pe.matmul(o, qkv_x[:, 128 * n:128 * n + 128], sb_member[:, NT, :], start=False, stop=True)
                ins.then_inc(S["qkl_ps"], 1)
                pe.wait_ge(S["qlbd_ready"], b + 1)
                pe.wait_ge(S["qkxt_sb"], b + 1)
                for p in range(PAIRS):
                    half, q = p // 4, 2 * (p % 4)
                    ins = pe.matmul(ps[:, 4, LM * p:LM * p + LM], ql_bd[:, half, q:q + 2, :].rearrange("p h j -> p (h j)"),
                                    klt[:, half, :], start=True, stop=True)
                ins.then_inc(S["s2_ps"], 1)
                for bank, part, t, half in ((6, 2, ql_bd, 0), (7, 3, ql_bd, 1), (2, 0, kl_bd, 0), (5, 1, kl_bd, 1)):
                    if bank == 2:
                        pe.wait_ge(S["klbd_ready"], b + 1)
                    pe.matmul(ps[:, bank, :], mt[:, part, :], t[:, half, :, :].rearrange("p h j -> p (h j)"),
                              start=True, stop=True).then_inc(S["g_ps"], 1)
                pe.wait_ge(S["xbd_ready"], b + 1)
                pe.wait_ge(S["coef_act"], 5 * b + 5)
                pe.wait_ge(S["coef_dve"], 4 * b + 4)
                for i in range(2):
                    for j in range(4):
                        ins = pe.transpose(ps[:, i, 128 * j:128 * j + 128], xbd[:, 4 * i + j, :], ident)
                    ins.then_inc(S["xt_ps"], 1)

            def pseudo_inverse(b):
                act_n, dve_n = [0, 0], [0, 0]

                def unit(u):
                    p, k = UNITS[u]
                    if u == 0:
                        pe.wait_ge(S["g_ready"], 4 * b + 2)
                    if u >= 2:
                        pe.wait_ge(S["s3m_used"], len(UNITS) * b + u - 1)
                    if p is None:
                        for j in range(4):
                            ins = pe.matmul(ps[:, 6 + u % 2, 128 * j:128 * j + 128],
                                            ql_bd[:, k, 2 * j:2 * j + 2, :].rearrange("p h j -> p (h j)"),
                                            qk_xt[:, 2 + k, :], start=True, stop=True)
                    else:
                        ins = pe.matmul(ps[:, 6 + u % 2, :], g3[:, 128 * p:128 * p + 128],
                                        coef_t[:, 512 * k:512 * k + 512], start=True, stop=True)
                    ins.then_inc(S["s3m_pe"], 1)

                def tile(n):
                    if n == 0:
                        pe.wait_ge(S["g3_shift"], b + 1)
                    for i in range(2):
                        if n:
                            pe.wait_ge(S[f"s3_exp{i}"], TILES * b + n)
                        ins = pe.matmul(ps[:, 6 + i, :], coef_t[:, 128 * n:128 * n + 128], g3[:, 512 * i:512 * i + 512],
                                        start=True, stop=n < NT)
                        if n == NT:
                            ins = pe.matmul(ps[:, 6 + i, :], qk_xt[:, 2 + i, :],
                                            ql_bd[:, i, :, :].rearrange("p h j -> p (h j)"), start=False, stop=True)
                        ins.then_inc(S[f"s3_pe{i}"], 1)
                    if n and n % 2 == 0:
                        for m in (n - 2, n - 1):
                            for i in range(2):
                                q = 2 * (m % 2) + i
                                ins = pe.matmul(ps[32 * q:32 * q + 32, 5, :], cf[:, m, :],
                                                p3[:, m % 4, 512 * i:512 * i + 512], start=n == 2, stop=n == NT,
                                                skip_group_check=True)
                        ins.then_inc(S["pv3_pe"], 1)

                pe.wait_ge(S["xt_sb"], 2 * b + 2)
                def fill(work):
                    for kind, what in work:
                        if kind == "unit":
                            unit(what)
                        elif kind == "shift":
                            pe.wait_ge(S["m3_ready"], b + 1)
                            for p in range(PAIRS):
                                ins = pe.matmul(ps[32:64, 6 + p // 4, 128 * (p % 4):128 * (p % 4) + 128], m3z[:, p, :],
                                                ident, start=True, stop=True)
                            ins.then_inc(S["m3_ps"], 1)
                        elif kind == "tile":
                            tile(what)
                        elif kind == "row":
                            row_scores(b, 0, what)

                for s, k, half, within, after in pinv_steps():
                    def product(i, lhs, rhs, done=False):
                        for j in range(4):
                            n = 4 * half + j
                            ins = pe.matmul(pinv_bank(half, i)[:, j, :], lhs[:, n, :], rhs[:, n, :],
                                            start=True, stop=True)
                        if done:
                            ins.then_inc(S[f"pi_pe{half}"], 1)

                    def turn():
                        pe.wait_ge(S[f"pi_act{1 - half}"], past(PI_ACT * b + act_n[1 - half]))

                    pe.wait_ge(S[f"pi_act{half}"], past(PI_ACT * b + act_n[half]))
                    pe.wait_ge(S[f"pi_dve{half}"], past(PI_DVE * b + dve_n[half]))
                    if s == "init":
                        product(0, xt, xbd)
                        product(1, xbd, xt, True)
                        act_n[half] += 2
                        dve_n[half] += 1
                    elif s == "square":
                        product(0, ym, yt, True)
                        act_n[half] += 1
                    elif s == "poly":
                        product(1, y2t, y7, True)
                        dve_n[half] += 1
                    elif k < ITERS - 1:
                        if k == 0:
                            pe.wait_ge(S["g_ready"], 4 * b + 3 + half)
                        product(0, yt, qm)
                        fill(sum(within[:1], []))
                        product(1, qm, yt)
                        fill(sum(within[1:], []))
                        turn()
                        product(2, qm, vt if k else xt, True)
                        act_n[half] += 3
                        dve_n[half] += 1
                    else:
                        turn()
                        product(2, qm, vt, True)
                        act_n[half] += 1
                    fill(after)
                for half in range(2):
                    pe.wait_ge(S[f"pi_act{half}"], past(PI_ACT * (b + 1)))

            def landmark_values(b):
                for i in range(2):
                    pe.wait_ge(S[f"s3_exp{i}"], TILES * (b + 1))
                for i in range(2):
                    ins = pe.matmul(ps[32 * i:32 * i + 32, 5, :], cf[:, NT, :], p3[:, 0, 512 * i:512 * i + 512],
                                    start=False, stop=True, skip_group_check=True)
                ins.then_inc(S["pv3_pe"], 1)
                pe.wait_ge(S["c3_sb"], b + 1)
                for p in range(PAIRS):
                    o = ps[:, 4, 34 * p:34 * p + 34]
                    pe.matmul(o, c3[:, 128 * (p % 4):128 * (p % 4) + 128], v4x[:, p, :], start=True, stop=True)
                    ins = pe.matmul(o[:, 0:32], p3[:, 0, 128 * p:128 * p + 128], qkv_x[:, 512 + 32 * p:544 + 32 * p],
                                    start=False, stop=True, skip_group_check=True)
                ins.then_inc(S["o3_ps"], 1)
                max_rows(b, 0, 4)
                pe.wait_ge(S["w3_ready"], b + 1)
                for p in range(PAIRS):
                    ins = pe.matmul(ps[:, 6, 16 * p:16 * p + 16], vt[:, p, :], w3[:, p, :], start=True, stop=True)
                ins.then_inc(S["z_ps"], 1)
                pe.wait_ge(S["z_ready"], b + 1)

            def row_scores(b, k, j):
                t = 4 * (C9 * b + k) + j
                if not first(t):
                    pe.wait_ge(S["s1m_used"], past(t))
                for i in range(2):
                    ins = pe.matmul(ps[:, i, :], coef_t[:, ds(512 * k + 128 * j, 128)], g1[:, 512 * i:512 * i + 512],
                                    start=True, stop=True)
                ins.then_inc(S["s1m_pe"], 1)

            def text_row_scores(b):
                pe.wait_ge(S["s1m_used"], past(4 * (C9 * b + CH)))
                for i in range(2):
                    ins = pe.matmul(ps[:, i, :], qk_xt[:, i, :], kl_bd[:, i, :, :].rearrange("p h j -> p (h j)"),
                                    start=True, stop=True)
                ins.then_inc(S["s1m_pe"], 4)

            def max_rows(b, k, n):
                c = C9 * b + k
                pe.wait_ge(S["s1m_used"], past(4 * c + 4))
                for j in range(n):
                    ins = pe.transpose(psb(0)[MAXROW:MAXROW + H, 128 * j:128 * j + 128], m1[:, j, :], identb[:, :])
                ins.then_inc(S["m1t_ps"], 1)

            def scores(b, k, g, pps, w, text):
                c = C9 * b + k
                for pp in pps:
                    e = 8 * c + 4 * g + pp
                    p = 4 * g + pp
                    if not (isinstance(k, int) and k == 0 and g == 0 and pp < 2):
                        pe.wait_ge(S["p1_ready"], e - 1)
                    o = ps[:, 2 + pp % 2, 0:w]
                    ins = pe.matmul(o, g1[:, 128 * p:128 * p + 128], coef_t[:, ds(512 * k, w)], start=True, stop=not text)
                    if text:
                        ins = pe.matmul(o, kl_bd[:, g, 2 * pp:2 * pp + 2, :].rearrange("p h j -> p (h j)"),
                                        qk_xt[:, g, :], start=False, stop=True)
                    ins.then_inc(S["s1_pe"], 1)

            def values(b, k, g, w):
                c = C9 * b + k
                pe.wait_ge(S["p1_ready"], 8 * c + 4 * g + 4)
                pe.wait_ge(S["u_ready"], past(2 * c + g))
                if g == 0:
                    pe.wait_ge(S["d_ready"], past(c))
                for q in range(4):
                    pe.matmul(ps[32 * q:32 * q + 32, 4, 0:w], z_bd[:, 4 * g + q, :], p1[:, g, q, 0:w],
                              start=True, stop=True)
                for q in range(4):
                    a = LAYOUT["onehot"][0] + 32 * (4 * g + q)
                    ins = pe.matmul(ps[32 * q:32 * q + 32, 5, 0:w], sb_const[:, a:a + 32], p1[:, g, q, 0:w],
                                    start=g == 0, stop=g == 1, skip_group_check=True)
                ins.then_inc(S["ud_pe"], 1)

            def turn_denominators(b, kp, n):
                cp = C9 * b + kp
                pe.wait_ge(S["d_ready"], past(cp + 1))
                for j in range(n):
                    ins = pe.transpose(ps[:, 7, 128 * j:128 * j + 128], d_sb[:, 128 * j:128 * j + 128], ident)
                ins.then_inc(S["dt_ps"], 1)

            def turn_reciprocals(b, kp, g, n):
                cp = C9 * b + kp
                pe.wait_ge(S["rdb_ready"], past(cp + 1))
                pe.wait_ge(S["o_ready"], 2 * cp + g) if g else pe.wait_ge(S["dt_used"], cp + 1)
                for j in range(n):
                    ins = pe.transpose(ps[:, 7, 128 * j:128 * j + 128],
                                       rd_all[:, j, 8 * g:8 * g + 8, :].rearrange("p h d -> p (h d)"), ident)
                ins.then_inc(S["rdt_ps"], 1)

            def project(b, kp, i, tiles, text=False):
                cp = C9 * b + kp
                if tiles[0] == 0:
                    pe.wait_ge(S["o_ready"], 2 * cp + 2)
                    pe.wait_ge(S["out_ready"], past(2 * cp + i))
                for jj in tiles:
                    j = 2 * i + jj
                    o = ps[:, 6, 256 * jj:256 * jj + 256]
                    if not text:
                        pe.matmul(o, coef_t[:, ds(512 * kp + 128 * j, 128)], res_w[:, :], start=True, stop=False)
                    for g in range(2):
                        ins = pe.matmul(o, o_sb[:, g, 128 * j:128 * j + 128], wo[:, g, :], start=text and g == 0,
                                        stop=g == 1)
                if text or tiles[-1] == 1:
                    ins.then_inc(S["out_ps"], 2 if text else 1)

            def chunk(b, k, w, prev, before, nxt):
                text = isinstance(k, int) and k == CH
                text_next = nxt and isinstance(k, int) and k == CH - 1
                rows = nxt and not text_next
                if prev:
                    turn_denominators(b, k - 1, 4)
                pe.wait_ge(S["m1t_sb"], C9 * b + k + 1)
                scores(b, k, 0, (0, 1), w, text)
                if text_next:
                    text_row_scores(b)
                elif rows:
                    row_scores(b, k + 1, 0)
                if before:
                    project(b, k - 2, 1, (0, 1))
                scores(b, k, 0, (2, 3), w, text)
                if prev:
                    turn_reciprocals(b, k - 1, 0, 4)
                scores(b, k, 1, (0,), w, text)
                if rows:
                    row_scores(b, k + 1, 1)
                values(b, k, 0, w)
                scores(b, k, 1, (1,), w, text)
                if prev:
                    turn_reciprocals(b, k - 1, 1, 4)
                if rows:
                    row_scores(b, k + 1, 2)
                scores(b, k, 1, (2,), w, text)
                scores(b, k, 1, (3,), w, text)
                if prev:
                    project(b, k - 1, 0, (0,))
                if rows:
                    row_scores(b, k + 1, 3)
                values(b, k, 1, w)
                if nxt:
                    max_rows(b, k + 1, 1 if text_next else 4)
                if prev:
                    project(b, k - 1, 0, (1,))

            def batch(b):
                pe.wait_ge(S["out_ready"], past(2 * C9 * b))
                setup_sequence(b)
                pseudo_inverse(b)
                landmark_values(b)
                chunk(b, 0, 512, False, False, True)
                chunk(b, 1, 512, True, False, True)
                with pe.Fori(1, CH // 2 - 1) as i:
                    chunk(b, 2 * i, 512, True, True, True)
                    chunk(b, 2 * i + 1, 512, True, True, True)
                chunk(b, CH - 2, 512, True, True, True)
                chunk(b, CH - 1, 512, True, True, True)
                chunk(b, CH, P, True, True, False)
                project(b, CH - 1, 1, (0, 1))
                turn_denominators(b, CH, 1)
                turn_reciprocals(b, CH, 0, 1)
                turn_reciprocals(b, CH, 1, 1)
                project(b, CH, 0, (0,), True)

            with pe.Fori(0, NB) as b:
                batch(b)

            pe.wait_ge(S["out_ready"], past(2 * C9 * NB))
            pe.wait_ge(S["f_we"], 1)
            for i in range(4):
                for j in range(4):
                    ins = pe.transpose(psb(i)[:, 128 * j:128 * j + 128], wt[:, 4 * i + j, :], identb[:, :])
                ins.then_inc(S["f_wet_ps"], 1)

            def turn_rows(c):
                pe.wait_ge(S["f_xn"], c + 1)
                for i in range(2):
                    for k in range(2):
                        for j in range(2):
                            ins = pe.transpose(ps[:, 6 + i, 256 * k + 128 * j:256 * k + 128 * j + 128],
                                               xn[:, 2 * i + j, 128 * k:128 * k + 128], ident)
                    ins.then_inc(S["f_xnt_ps"], 1)

            def out_rows(c):
                pe.wait_ge(S["f_y2"], 4 * c + 4)
                for i in range(2):
                    for jj in range(2):
                        for p in range(E // 2):
                            a = 128 * (2 * i + jj)
                            ins = pe.matmul(ps[:, 6 + i, 256 * jj:256 * jj + 256], y2[:, p, a:a + 128], w2b_s[:, p, :],
                                            start=p == 0, stop=p == 3)
                    ins.then_inc(S["f_out_ps"], 1)

            def experts(c, last):
                pe.wait_ge(S["f_xnt"], 2 * c + 2)
                for p in range(E // 2):
                    if p >= 2:
                        pe.wait_ge(S["f_mid"], 4 * c + p - 1)
                    elif not first(c):
                        pe.wait_ge(S["f_y2"], 4 * c - 1 + p)
                    for k in range(2):
                        ins = pe.matmul(ps[:, 4 + p % 2, :], w1a_s[:, k, 128 * p:128 * p + 128], xn_t[:, k, :],
                                        start=k == 0, stop=k == 1)
                    ins.then_inc(S["f_l0"], 1)
                if not first(c):
                    out_rows(c - 1)
                for p in range(E // 2):
                    if not (first(c) and p == 0):
                        pe.wait_ge(S["f_wx"], 4 * c + p)
                    if p == 0 and not first(c):
                        pe.wait_ge(S["f_out"], 2 * c - 1)
                    if p == 3 and not last:
                        pe.wait_ge(S["f_xnt"], 2 * c + 3)
                    pe.matmul(ps[:, 6, :], sel_e[:, 128 * p:128 * p + 128], we_t[:, ds(512 * c, 512)],
                              start=True, stop=True).then_inc(S["f_wx_ps"], 1)
                    if p == 2 and not last:
                        pe.wait_ge(S["f_wx"], 4 * c + p + 1)
                        turn_rows(c + 1)
                    pe.wait_ge(S["f_mid"], 4 * c + p + 1 if p < 2 else 4 * c + 4)
                    if p < 2:
                        pe.wait_ge(S["f_mid"], 4 * c + p + 3)
                    else:
                        pe.wait_ge(S["f_y2"], 4 * c + p - 1)

                    def second(f):
                        u = (4 * c + p) * FB + f
                        pe.wait_ge(S["f_gelu"], 2 * u + 2)
                        for e in range(2):
                            a = 64 * (2 * p + e)
                            ins = pe.matmul(ps[64 * e:64 * e + 64, 4 + p % 2, :], w2a_s[:, f, a:a + 64],
                                            hid[:, e, f % 2, :], start=f == 0, stop=f == FB - 1)
                        ins.then_inc(S["f_l2"], 1)

                    for f in range(FB):
                        u = (4 * c + p) * FB + f
                        if not (first(c) and p == 0 and f < 2):
                            pe.wait_ge(S["f_gelu"], 2 * u - 2)
                        for e in range(2):
                            pe.matmul(ps[:, 2 * (f % 2) + e, :], w1b_z[:, 2 * p + e, 128 * f:128 * f + 128],
                                      mid[:, p, :], start=True, stop=True).then_inc(S["f_l1"], 1)
                        if f:
                            second(f - 1)
                    second(FB - 1)
            pe.wait_ge(S["f_in"], 16 * 5)
            pe.wait_ge(S["f_zero"], 2)
            turn_rows(0)
            pe.wait_ge(S["f_wet"], 4)
            experts(0, False)
            with pe.Fori(1, FT // 4 - 1) as c:
                experts(c, False)
            experts(FT // 4 - 1, True)
            out_rows(FT // 4 - 1)


def kernel(x, txt, L0_tok_kernel, L0_tok_bias, L0_attn_Wqkv, L0_attn_bqkv, L0_attn_Wout, L0_attn_bout,
           L0_ffn_expert_weights, L0_ffn_expert_indices, L0_ffn_w1_A, L0_ffn_w1_B, L0_ffn_w2_A, L0_ffn_w2_B):
    import concourse.bacc as bacc
    from concourse.bass_utils import run_bass_kernel_spmd

    consts, member = constants()
    arrays = {
        "x": np.asarray(x).reshape(NB, 2, P, 48), "txt": np.asarray(txt),
        "tok_kernel": np.asarray(L0_tok_kernel), "tok_bias": np.asarray(L0_tok_bias).reshape(1, D),
        "wqkv": np.asarray(L0_attn_Wqkv), "bqkv": np.asarray(L0_attn_bqkv).reshape(1, 3 * D),
        "wout": np.asarray(L0_attn_Wout), "bout": np.asarray(L0_attn_bout).reshape(1, D),
        "ew": np.asarray(L0_ffn_expert_weights).reshape(P, 2 * FT),
        "ei": np.asarray(L0_ffn_expert_indices).reshape(P, 2 * FT),
        "w1a_t": np.asarray(L0_ffn_w1_A).T, "w1b": np.asarray(L0_ffn_w1_B),
        "w2a_t": np.asarray(L0_ffn_w2_A).T, "w2b": np.asarray(L0_ffn_w2_B),
        "consts": consts, "member": member,
    }
    arrays = {k: np.ascontiguousarray(v) for k, v in arrays.items()}
    nc = bacc.Bacc("TRN2", target_bir_lowering=False, num_devices=1)
    args = [nc.dram_tensor(k, v.shape, mybir.dt.from_np(v.dtype), kind="ExternalInput").ap() for k, v in arrays.items()]
    out = nc.dram_tensor("out", (NB, NG + NX, D), F32, kind="ExternalOutput").ap()
    build(nc, *args, out)
    r = run_bass_kernel_spmd(nc, [arrays], core_ids=[0])
    return r.results[0]["out"]
```
